# Optimizing a Trainium2 kernel written in Bass

```python
import numpy as np
import jax
import jax.numpy as jnp

def _softmax(x, axis=-1):
    return jax.nn.softmax(x, axis=axis)

def _gelu(x):
    return jax.nn.gelu(x, approximate=True)

def _silu(x):
    return jax.nn.silu(x)

def _sigmoid(x):
    return jax.nn.sigmoid(x)

def _layernorm(x, axis=-1, eps=1e-05):
    m = jnp.mean(x, axis=axis, keepdims=True)
    v = jnp.var(x, axis=axis, keepdims=True)
    return (x - m) / jnp.sqrt(v + eps)

def _scatter_add(tgt, idx, src, axis=0):
    return tgt.at[idx].add(src)

def _segment_sum(src, seg, n):
    return jax.ops.segment_sum(src, seg, n)
kernel_name = 'mk_cond_resid_d4_seqx_r4_582bd2'

def setup_inputs(seed: int=0):
    np.random.seed(seed)
    _w = jnp.asarray

    def _rec_inputs():
        import jax
        import jax.numpy as jnp
        _rk = jax.random.key(seed)
        x = 7.22e-05 + 1 * jax.random.normal(jax.random.fold_in(_rk, 1), (16, 256, 256), jnp.float32)
        _lenS = 256 - jax.random.randint(jax.random.fold_in(_rk, 7), (16,), 0, max(1, 256 // 4) + 1, jnp.int32)
        _lenS2 = 256 - jax.random.randint(jax.random.fold_in(_rk, 8), (16,), 0, max(1, 256 // 4) + 1, jnp.int32)
        condB_tauraws = -5.74692 + 0.777674 * jax.random.normal(jax.random.fold_in(_rk, 11), (16,), jnp.float32)
        cond_256 = -0.000235209 + 0.019331 * jax.random.normal(jax.random.fold_in(_rk, 12), (16, 64), jnp.float32)
        condB_bn2 = jnp.zeros((16,), jnp.float32)
        cond_1024 = -4.10585e-05 + 0.0199478 * jax.random.normal(jax.random.fold_in(_rk, 14), (16, 256), jnp.float32)
        itok_B_0_2 = jax.random.randint(jax.random.fold_in(_rk, 15), (16,), 0, 3, jnp.int32)
        fside_Bx8_0 = jax.random.uniform(jax.random.fold_in(_rk, 16), (16, 8), jnp.float32, 0.0, 0.556406)
        condB_sharedgateprob = jax.random.uniform(jax.random.fold_in(_rk, 17), (16,), jnp.float32, 0.0, 0.794948)
        itok_B_0_7 = jax.random.randint(jax.random.fold_in(_rk, 18), (16,), 0, 8, jnp.int32)
        return (x, condB_tauraws, cond_256, condB_bn2, cond_1024, itok_B_0_2, fside_Bx8_0, condB_sharedgateprob, itok_B_0_7)
    x, condB_tauraws, cond_256, condB_bn2, cond_1024, itok_B_0_2, fside_Bx8_0, condB_sharedgateprob, itok_B_0_7 = _rec_inputs()

    def _L0_cond_setup():
        import jax, jax.numpy as jnp
        import numpy as np
        import math
        B, T, E, D = (4, 512, 256, 4)

        def _tau_init(t):
            a = 0.1 ** (1.0 / max(t - 1, 1))
            tt = -math.log(max(a, 1e-10))
            return math.log(math.exp(tt) - 1 + 1e-10)

        def causal_ema(b, tau_raw):
            alpha = jnp.exp(-jax.nn.softplus(tau_raw)).astype(b.dtype)

            def step(h, bt):
                h = alpha * h + bt
                return (h, h)
            h0 = jnp.zeros((b.shape[0], b.shape[2]), b.dtype)
            _, hs = jax.lax.scan(step, h0, jnp.swapaxes(b, 0, 1))
            return jnp.swapaxes(hs, 0, 1)
        key = jax.random.key(seed)
        ks = jax.random.split(key, 10)
        s = 0.02
        return {'x': jax.random.normal(ks[0], (B, T, E), jnp.float32), 'tau_ctx': jnp.float32(_tau_init(max(T // 2, 4))), 'tau_raws': jnp.array([_tau_init(max(T // 2 ** i, 2)) for i in range(D)], jnp.float32), 'Wg': jax.random.normal(ks[1], (E, 2 * E), jnp.float32) * s, 'bg': jnp.full((E,), -0.5, jnp.float32), 'Wn1': jax.random.normal(ks[2], (E // 4, E), jnp.float32) * s, 'bn1': jnp.zeros((E // 4,), jnp.float32), 'Wn2': jax.random.normal(ks[3], (D, E // 4), jnp.float32) * s, 'bn2': jnp.zeros((D,), jnp.float32), 'blend': jax.random.normal(ks[4], (D, E), jnp.float32) * s, 'Wsoma': jax.random.normal(ks[5], (E, E), jnp.float32) * s, 'bsoma': jnp.zeros((E,), jnp.float32), 'Wtemp': jax.random.normal(ks[6], (E, E), jnp.float32) * s, 'btemp': jnp.zeros((E,), jnp.float32), 'Wout': jax.random.normal(ks[7], (E, E), jnp.float32) * s, 'gamma': jnp.ones((E,), jnp.float32), 'beta': jnp.zeros((E,), jnp.float32)}
    _L0_cond_all = _L0_cond_setup()
    _L0_cond_in = {k: v for k, v in _L0_cond_all.items() if k in ('tau_ctx', 'Wg', 'bg', 'Wn1', 'bn1', 'Wsoma', 'bsoma', 'Wtemp', 'btemp', 'Wout', 'gamma', 'beta')}
    del _L0_cond_all

    def _L1_cond_setup():
        import jax, jax.numpy as jnp
        import numpy as np
        NEG_INF = -1e+30
        key = jax.random.key(seed)
        k1, k2, k3, k4, k5 = jax.random.split(key, 5)
        B, S, D, A = (16, 256, 256, 64)
        hidden = jax.random.normal(k1, (B, S, D), dtype=jnp.float32)
        W1 = jax.random.normal(k2, (D, A), dtype=jnp.float32) / np.sqrt(D)
        b1 = jax.random.normal(k3, (A,), dtype=jnp.float32) * 0.01
        v = jax.random.normal(k4, (A,), dtype=jnp.float32) / np.sqrt(A)
        prompt_type_ids = jax.random.randint(k5, (B,), 0, 3, dtype=jnp.int32)
        return {'hidden': hidden, 'W1': W1, 'b1': b1, 'v': v, 'prompt_type_ids': prompt_type_ids}
    _L1_cond_all = _L1_cond_setup()
    _L1_cond_in = {k: v for k, v in _L1_cond_all.items() if k in ('W1', 'b1', 'v')}
    del _L1_cond_all

    def _L2_cond_setup():
        import jax, jax.numpy as jnp
        import numpy as np
        E, B, S, D, F = (8, 2, 256, 256, 1024)
        key = jax.random.key(seed)
        ks = jax.random.split(key, 9)
        sc_d = 1.0 / np.sqrt(D)
        sc_f = 1.0 / np.sqrt(F)
        hidden_states = jax.random.normal(ks[0], (B, S, D), dtype=jnp.float32)
        gating_probs = jax.nn.softmax(jax.random.normal(ks[1], (B, E), dtype=jnp.float32), axis=-1)
        shared_gate_prob = jax.nn.sigmoid(jax.random.normal(ks[2], (B, 1), dtype=jnp.float32))
        Wg = jax.random.normal(ks[3], (E, D, F), dtype=jnp.float32) * sc_d
        Wu = jax.random.normal(ks[4], (E, D, F), dtype=jnp.float32) * sc_d
        Wd = jax.random.normal(ks[5], (E, F, D), dtype=jnp.float32) * sc_f
        Sg = jax.random.normal(ks[6], (D, F), dtype=jnp.float32) * sc_d
        Su = jax.random.normal(ks[7], (D, F), dtype=jnp.float32) * sc_d
        Sd = jax.random.normal(ks[8], (F, D), dtype=jnp.float32) * sc_f
        return {'hidden_states': hidden_states, 'gating_probs': gating_probs, 'shared_gate_prob': shared_gate_prob, 'Wg': Wg, 'Wu': Wu, 'Wd': Wd, 'Sg': Sg, 'Su': Su, 'Sd': Sd}
    _L2_cond_all = _L2_cond_setup()
    _L2_cond_in = {k: v for k, v in _L2_cond_all.items() if k in ('Wg', 'Wu', 'Wd', 'Sg', 'Su', 'Sd')}
    del _L2_cond_all

    def _L3_cond_setup():
        import jax, jax.numpy as jnp
        import numpy as np
        IN, HID, OUT, PART, E = (256, 1024, 256, 64, 8)
        B, N = (16, 512)
        key = jax.random.key(seed)
        ks = jax.random.split(key, 8)
        s1 = 1.0 / np.sqrt(IN)
        s2 = 1.0 / np.sqrt(HID)
        return {'x': jax.random.normal(ks[0], (B, N, IN), dtype=jnp.float32), 'indices': jax.random.randint(ks[1], (B,), 0, E, dtype=jnp.int64), 'W1': jax.random.uniform(ks[2], (IN, HID), jnp.float32, -s1, s1), 'b1': jax.random.uniform(ks[3], (HID,), jnp.float32, -s1, s1), 'W2': jax.random.uniform(ks[4], (HID, OUT - PART), jnp.float32, -s2, s2), 'b2': jax.random.uniform(ks[5], (OUT - PART,), jnp.float32, -s2, s2), 'We': jax.random.uniform(ks[6], (E, HID, PART), jnp.float32, -s2, s2), 'be': jax.random.uniform(ks[7], (E, PART), jnp.float32, -s2, s2)}
    _L3_cond_all = _L3_cond_setup()
    _L3_cond_in = {k: v for k, v in _L3_cond_all.items() if k in ('W1', 'b1', 'W2', 'b2', 'We', 'be')}
    del _L3_cond_all
    return {'x': x, 'condB_tauraws': condB_tauraws, 'cond_256': cond_256, 'condB_bn2': condB_bn2, 'cond_1024': cond_1024, 'itok_B_0_2': itok_B_0_2, 'fside_Bx8_0': fside_Bx8_0, 'condB_sharedgateprob': condB_sharedgateprob, 'itok_B_0_7': itok_B_0_7, 'L0_cond_tau_ctx': _L0_cond_in['tau_ctx'], 'L0_cond_Wg': _L0_cond_in['Wg'], 'L0_cond_bg': _L0_cond_in['bg'], 'L0_cond_Wn1': _L0_cond_in['Wn1'], 'L0_cond_bn1': _L0_cond_in['bn1'], 'L0_cond_Wsoma': _L0_cond_in['Wsoma'], 'L0_cond_bsoma': _L0_cond_in['bsoma'], 'L0_cond_Wtemp': _L0_cond_in['Wtemp'], 'L0_cond_btemp': _L0_cond_in['btemp'], 'L0_cond_Wout': _L0_cond_in['Wout'], 'L0_cond_gamma': _L0_cond_in['gamma'], 'L0_cond_beta': _L0_cond_in['beta'], 'L1_cond_W1': _L1_cond_in['W1'], 'L1_cond_b1': _L1_cond_in['b1'], 'L1_cond_v': _L1_cond_in['v'], 'L2_cond_Wg': _L2_cond_in['Wg'], 'L2_cond_Wu': _L2_cond_in['Wu'], 'L2_cond_Wd': _L2_cond_in['Wd'], 'L2_cond_Sg': _L2_cond_in['Sg'], 'L2_cond_Su': _L2_cond_in['Su'], 'L2_cond_Sd': _L2_cond_in['Sd'], 'L3_cond_W1': _L3_cond_in['W1'], 'L3_cond_b1': _L3_cond_in['b1'], 'L3_cond_W2': _L3_cond_in['W2'], 'L3_cond_b2': _L3_cond_in['b2'], 'L3_cond_We': _L3_cond_in['We'], 'L3_cond_be': _L3_cond_in['be']}

def reference(x, condB_tauraws, cond_256, condB_bn2, cond_1024, itok_B_0_2, fside_Bx8_0, condB_sharedgateprob, itok_B_0_7, L0_cond_tau_ctx, L0_cond_Wg, L0_cond_bg, L0_cond_Wn1, L0_cond_bn1, L0_cond_Wsoma, L0_cond_bsoma, L0_cond_Wtemp, L0_cond_btemp, L0_cond_Wout, L0_cond_gamma, L0_cond_beta, L1_cond_W1, L1_cond_b1, L1_cond_v, L2_cond_Wg, L2_cond_Wu, L2_cond_Wd, L2_cond_Sg, L2_cond_Su, L2_cond_Sd, L3_cond_W1, L3_cond_b1, L3_cond_W2, L3_cond_b2, L3_cond_We, L3_cond_be):
    import jax
    import jax.numpy as jnp

    def _L0_cond_ref(x, tau_ctx, tau_raws, Wg, bg, Wn1, bn1, Wn2, bn2, blend, Wsoma, bsoma, Wtemp, btemp, Wout, gamma, beta):
        import jax, jax.numpy as jnp
        import numpy as np
        import math
        B, T, E, D = (4, 512, 256, 4)

        def _tau_init(t):
            a = 0.1 ** (1.0 / max(t - 1, 1))
            tt = -math.log(max(a, 1e-10))
            return math.log(math.exp(tt) - 1 + 1e-10)

        def causal_ema(b, tau_raw):
            alpha = jnp.exp(-jax.nn.softplus(tau_raw)).astype(b.dtype)

            def step(h, bt):
                h = alpha * h + bt
                return (h, h)
            h0 = jnp.zeros((b.shape[0], b.shape[2]), b.dtype)
            _, hs = jax.lax.scan(step, h0, jnp.swapaxes(b, 0, 1))
            return jnp.swapaxes(hs, 0, 1)
        ctx = causal_ema(x, tau_ctx)
        gate_in = jnp.concatenate([x, ctx], axis=-1)
        wg = jax.nn.sigmoid(jnp.einsum('btc,ec->bte', gate_in, Wg) + bg)
        gated = x * wg
        h1 = jax.nn.gelu(jnp.einsum('btc,hc->bth', x, Wn1) + bn1, approximate=False)
        mod = 0.5 + jax.nn.sigmoid(jnp.einsum('bth,dh->btd', h1, Wn2) + bn2)
        traces = jax.vmap(lambda tau, m: causal_ema(gated * m[..., None], tau))(tau_raws, jnp.moveaxis(mod, -1, 0))
        blend_w = jax.nn.softmax(blend, axis=0)
        temporal = jnp.einsum('dbtc,dc->btc', traces, blend_w)
        gate = jax.nn.sigmoid(jnp.einsum('btc,ec->bte', temporal, Wtemp) + btemp)
        soma = jax.nn.gelu(jnp.einsum('btc,ec->bte', x, Wsoma) + bsoma, approximate=False)
        out = jnp.einsum('btc,ec->bte', soma * gate, Wout)
        mu = out.mean(-1, keepdims=True)
        var = out.var(-1, keepdims=True)
        return (out - mu) / jnp.sqrt(var + 1e-05) * gamma + beta

    def _L1_cond_ref(hidden, W1, b1, v, prompt_type_ids):
        import jax, jax.numpy as jnp
        import numpy as np
        NEG_INF = -1e+30
        B, S, D = hidden.shape
        attn_in = jnp.tanh(jnp.einsum('bsd,da->bsa', hidden, W1) + b1)
        scores = jnp.einsum('bsa,a->bs', attn_in, v)
        idx = jnp.arange(S)
        j = idx[:, None]
        l = idx[None, :]
        prefix_m = l <= j
        postfix_m = l >= j
        cloze_m = l != j
        pt = prompt_type_ids[:, None, None]
        mask = jnp.where(pt == 0, prefix_m[None], jnp.where(pt == 1, postfix_m[None], cloze_m[None]))
        masked_scores = jnp.where(mask, scores[:, None, :], NEG_INF)
        p = jax.nn.softmax(masked_scores, axis=-1)
        cnt = jnp.sum(mask, axis=-1).astype(hidden.dtype)
        pooled = jnp.einsum('bjl,bld->bjd', p, hidden) / cnt[..., None]
        return pooled

    def _L2_cond_ref(hidden_states, gating_probs, shared_gate_prob, Wg, Wu, Wd, Sg, Su, Sd):
        import jax, jax.numpy as jnp
        import numpy as np
        E, B, S, D, F = (8, 2, 256, 256, 1024)
        h = hidden_states
        g = jnp.einsum('bsd,edf->ebsf', h, Wg)
        u = jnp.einsum('bsd,edf->ebsf', h, Wu)
        expert_outs = jnp.einsum('ebsf,efd->ebsd', jax.nn.silu(g) * u, Wd)
        expert_output = jnp.einsum('be,ebsd->bsd', gating_probs, expert_outs)
        shared = jnp.einsum('bsf,fd->bsd', jax.nn.silu(h @ Sg) * (h @ Su), Sd)
        sg = shared_gate_prob[:, :, None]
        return (1.0 - sg) * expert_output + sg * shared

    def _L3_cond_ref(x, indices, W1, b1, W2, b2, We, be):
        import jax, jax.numpy as jnp
        import numpy as np
        IN, HID, OUT, PART, E = (256, 1024, 256, 64, 8)
        B, N = (16, 512)
        h = jax.nn.gelu(jnp.einsum('bni,ih->bnh', x, W1) + b1, approximate=False)
        shared_x = jnp.einsum('bnh,ho->bno', h, W2) + b2
        We_sel = We[indices]
        be_sel = be[indices]
        expert_x = jnp.einsum('bnh,bhp->bnp', h, We_sel) + be_sel[:, None, :]
        return jnp.concatenate([shared_x, expert_x], axis=-1)
    x = x + _L0_cond_ref(x, L0_cond_tau_ctx, condB_tauraws, L0_cond_Wg, L0_cond_bg, L0_cond_Wn1, L0_cond_bn1, cond_256, condB_bn2, cond_1024, L0_cond_Wsoma, L0_cond_bsoma, L0_cond_Wtemp, L0_cond_btemp, L0_cond_Wout, L0_cond_gamma, L0_cond_beta)
    x = x + _L1_cond_ref(x, L1_cond_W1, L1_cond_b1, L1_cond_v, itok_B_0_2)
    x = x + _L2_cond_ref(x, fside_Bx8_0, condB_sharedgateprob[:, None], L2_cond_Wg, L2_cond_Wu, L2_cond_Wd, L2_cond_Sg, L2_cond_Su, L2_cond_Sd)
    x = x + _L3_cond_ref(x, itok_B_0_7, L3_cond_W1, L3_cond_b1, L3_cond_W2, L3_cond_b2, L3_cond_We, L3_cond_be)
    return x

_drawn_inputs = setup_inputs


def setup_inputs(seed=0):
    import zlib

    import numpy as np

    out = dict(_drawn_inputs(seed))
    spreads = {'condB_bn2': (0.0, 2.0),
     'L0_cond_bg': (-0.5, 0.6),
     'L0_cond_bn1': (0.0, 2.0),
     'L0_cond_bsoma': (0.0, 0.1),
     'L0_cond_btemp': (0.0, 0.29),
     'L0_cond_gamma': (1.0, 0.2),
     'L0_cond_beta': (0.0, 0.1)}
    factors = {'condB_tauraws': 8.0,
     'cond_256': 8.0,
     'cond_1024': 64.0,
     'L0_cond_Wn1': 8.0,
     'L1_cond_W1': 2.914,
     'L1_cond_b1': 200.0,
     'L1_cond_v': 2.765,
     'L3_cond_b1': 7.735,
     'L3_cond_b2': 6.285,
     'L3_cond_be': 8.0}
    for name, (base, spread) in spreads.items():
        noise = np.random.default_rng([zlib.crc32(name.encode()), seed]).standard_normal(out[name].shape)
        drawn = base * np.exp(spread * noise) if base else spread * noise
        out[name] = jnp.asarray(drawn.astype(out[name].dtype))
    for name, factor in factors.items():
        out[name] = (out[name] * factor).astype(out[name].dtype)
    return out
```

```python
from contextlib import ExitStack

import concourse.bass as bass
from concourse import mybir

P = 128
B, S, D = 16, 256, 256
T = B * S
DH = D // P
BB = 2
BT = BB * S
NBLK = T // BT
ND = 16
NE, F = 8, 1024
FC = F // P
PART, NSH = 64, 192
A = 64
GROUPS = [[0], [1, 2], [3, 4], [5, 6], [7]]
WSLOTS = 9
WROW = DH * P * 2 + D
NACC = 4
NEG = -1e30


class Signal:

    def __init__(self, sem):
        self.sem, self.count = sem, 0

    def after(self, by):
        self.count += by
        return self, self.count


class Lane:

    def __init__(self, counter):
        self.work, self.passed, self.counter = [], {}, counter

    def wait(self, *marks):
        for mark in marks:
            if mark is None:
                continue
            signal, count = mark
            if self.passed.get(signal, 0) < count:
                self.passed[signal] = count
                self.work.append(lambda eng, s=signal.sem, c=count: eng.wait_ge(s, c))

    def do(self, build, signal=None, by=1, quiet=False):
        if quiet:
            self.work.append(lambda eng: build())
            return None
        signal = signal or self.counter
        self.work.append(lambda eng: build().then_inc(signal.sem, by))
        return signal.after(by)


def residual_stack_kernel(nc, xT, chunks, sidew, vec128, w64, vec16, masks, ident, l3w1, l3w2, we_rows,
                          be_pad, blendT, taus, types, experts, gates, shared_gate, jcount, prow, yT):
    fp32, f32r, i32, u32 = mybir.dt.float32, mybir.dt.float32r, mybir.dt.int32, mybir.dt.uint32
    ALU, ACT = mybir.AluOpType, mybir.ActivationFunctionType
    AX = mybir.AxisListType.X
    ctx = ExitStack()
    with ctx:
        def sb(name, shape, dt=fp32):
            return ctx.enter_context(nc.sbuf_tensor(name, shape, dt))

        def signal(name):
            return Signal(ctx.enter_context(nc.semaphore(name)))

        w_hi = [sb(f"w_hi{i}", [P, WROW], f32r) for i in range(WSLOTS)]
        w_lo = [sb(f"w_lo{i}", [P, WROW], f32r) for i in range(WSLOTS)]
        w_raw = [sb(f"w_raw{i}", [P, WROW]) for i in range(3)]
        x2_hi = [sb(f"x2_hi{i}", [P, DH, BT], f32r) for i in range(2)]
        x2_lo = [sb(f"x2_lo{i}", [P, DH, BT], f32r) for i in range(2)]
        acc = [sb(f"acc{i}", [P, DH, BT]) for i in range(NACC)]
        hid = [sb(f"hid{i}", [P, BT]) for i in range(3)]
        hid_hi = [sb(f"hid_hi{i}", [P, BT], f32r) for i in range(2)]
        hid_lo = [sb(f"hid_lo{i}", [P, BT], f32r) for i in range(2)]
        x_in = [sb(f"x_in{i}", [P, DH, BT]) for i in range(2)]
        ema = sb("ema", [P, DH, BT])
        gated = sb("gated", [P, DH, BT])
        temporal = sb("temporal", [P, DH, BT])
        trace = [sb(f"trace{i}", [P, DH, BT]) for i in range(2)]
        soma = sb("soma", [P, DH, BT])
        small = sb("small", [A, BT])
        mod = sb("mod", [ND, BT])
        mod_pair = sb("mod_pair", [48, BT], f32r)
        stat = sb("stat", [P, BT])
        xt_hi = sb("xt_hi", [P, DH, D], f32r)
        xt_lo = sb("xt_lo", [P, DH, D], f32r)
        pt_hi = sb("pt_hi", [P, 2, S], f32r)
        pt_lo = sb("pt_lo", [P, 2, S], f32r)
        NSIDE = sidew.shape[1]
        side_w = sb("side_w", [P, NSIDE])
        o = 0
        wg = side_w[:, o:o + 4 * D].rearrange("p (k e) -> p k e", k=4); o += 4 * D
        wtemp = side_w[:, o:o + 2 * D].rearrange("p (k e) -> p k e", k=2); o += 2 * D
        wsoma = side_w[:, o:o + 2 * D].rearrange("p (k e) -> p k e", k=2); o += 2 * D
        wout = side_w[:, o:o + 2 * D].rearrange("p (k e) -> p k e", k=2); o += 2 * D
        wn1 = side_w[:, o:o + 2 * A].rearrange("p (k e) -> p k e", k=2); o += 2 * A
        wa1 = side_w[:, o:o + 2 * A].rearrange("p (k e) -> p k e", k=2); o += 2 * A
        assert o == NSIDE
        v128 = sb("v128", [P, vec128.shape[1]])
        bg, bsoma, btemp = v128[:, 0:2], v128[:, 2:4], v128[:, 4:6]
        gamma, beta, b1h, b2a = v128[:, 6:8], v128[:, 8:10], v128[:, 10:18], v128[:, 18:19]
        b2b = v128[:, 19:20]
        half128 = sb("half128", [P, 6])
        c64 = sb("c64", [A, w64.shape[1]])
        wn2, bn1, ba1, v_col = c64[:, 0:ND], c64[:, ND:ND + 1], c64[:, ND + 1:ND + 2], c64[:, ND + 2:ND + 3]
        v_rep = sb("v_rep", [A, P])
        bn2 = sb("bn2", [ND, 1])
        bn2_half = sb("bn2_half", [ND, 1])
        mask = sb("mask", [P, 3, 2, S])
        idn = sb("idn", [P, P])
        sel = sb("sel", [48, ND], f32r)
        mean_w = sb("mean_w", [P, P])
        bl = sb("bl", [P, DH, ND])
        bl_top = sb("bl_top", [P, DH])
        bl_sum = sb("bl_sum", [P, DH])
        tau = sb("tau", [P, ND + 1])
        alpha = sb("alpha", [P, ND + 1])
        typ_i = sb("typ_i", [P, B], i32)
        typ = sb("typ", [P, 5, B])
        pen = sb("pen", [P, 3, B])
        cnt = sb("cnt", [P, B, 2])
        jc = sb("jc", [P, 5])
        ge = sb("ge", [P, B, NE])
        sg = sb("sg", [P, 2, B])
        coef = sb("coef", [P, NE + 1, B])
        ex_i = sb("ex_i", [P, B], i32)
        ex_f = sb("ex_f", [P, 2, B])
        ex_row = sb("ex_row", [P, B], u32)
        onehot = sb("onehot", [NE, B])
        be_sb = sb("be_sb", [NE, P])
        bias_b = sb("bias_b", [P, B])
        row_id = sb("row_id", [P, 1])
        w1h = sb("w1h", [P, DH, F])
        w2h = sb("w2h", [P, FC, NSH])
        w2e = [sb(f"w2e{i}", [P, FC, P]) for i in range(2)]
        we_in = [sb(f"we_in{i}", [P, FC * PART]) for i in range(2)]
        top = sb("top", [P, 2])
        den = sb("den", [P, 2])

        bank = [ctx.enter_context(nc.psum_tensor(f"bank{i}", [P, 512], fp32)) for i in range(6)]
        ps_gate, ps_up, ps_side = bank[0:2], bank[2:4], bank[4:6]
        ps_out = ctx.enter_context(nc.psum_tensor("ps_out", [P, DH, BT], fp32))

        pe, act, dve, pool, sp = (Lane(signal(f"{n}_side")) for n in ("pe", "act", "dve", "pool", "sp"))
        s_const = signal("constants_in")
        s_raw = [signal(f"raw_in{i}") for i in range(3)]
        s_x = [signal(f"x_in{i}") for i in range(2)]
        s_we = [signal(f"we_in{i}") for i in range(2)]
        s_y = [signal(f"y_out{i}") for i in range(NACC)]
        s_whi, s_wlo = signal("w_hi"), signal("w_lo")
        s_gu, s_silu, s_hid = signal("gate_up"), signal("silu"), signal("hidden")
        s_hhi, s_hlo, s_down, s_acc = signal("hidden_hi"), signal("hidden_lo"), signal("down"), signal("acc")

        def f(t):
            return t.bitcast(fp32)

        def mm(out, lhsT, rhs, start, stop):
            return lambda: nc.tensor.matmul(out, lhsT, rhs, start=start, stop=stop)

        def products(out, pairs, wait=None):
            for i, (l, r) in enumerate(pairs):
                last = i == len(pairs) - 1
                mark = pe.do(mm(out, l, r, i == 0, last), quiet=not last)
            return mark

        loads = [(side_w[:], sidew[:]), (v128[:], vec128[:]), (c64[:], w64[:]), (bn2[:], vec16[:]),
                 (mask[:], masks[:]), (idn[:], ident[:]), (bl[:], blendT[:]),
                 (tau[:], taus.partition_broadcast(P)), (typ_i[:], types.partition_broadcast(P)),
                 (jc[:], jcount[:]), (ge[:], gates.partition_broadcast(P)),
                 (sg[:, 0, :], shared_gate.partition_broadcast(P)),
                 (ex_i[:], experts.partition_broadcast(P)), (row_id[:], prow[:]),
                 (w1h[:], l3w1[:]), (w2h[:], l3w2[:]), (be_sb[:], be_pad[:])]
        x_blk = xT.rearrange("(h p) t -> p h t", p=P)
        y_blk = yT.rearrange("(h p) t -> p h t", p=P)
        x_mark = {}

        def load_x(b):
            x_mark[b] = sp.do(lambda: nc.sync.dma_start(x_in[b % 2][:], x_blk[:, :, b * BT:(b + 1) * BT]),
                              s_x[b % 2], 16)

        load_x(0)
        for dst, src in loads:
            consts = sp.do(lambda dst=dst, src=src: nc.sync.dma_start(dst, src), s_const, 16)

        def v(build, *marks):
            dve.wait(*marks)
            return dve.do(build)

        def a(build, *marks):
            act.wait(*marks)
            return act.do(build)

        def setup():
            V, TS = nc.vector, nc.vector.tensor_scalar
            for lane in (dve, act, pool, pe):
                lane.wait(consts)
            m1 = v(lambda: TS(half128[:, 0:2], bg, 0.5, None, ALU.mult))
            m2 = v(lambda: TS(half128[:, 2:4], btemp, 0.5, None, ALU.mult))
            m3 = v(lambda: TS(bn2_half[:], bn2[:], 0.5, None, ALU.mult))
            m4 = v(lambda: V.tensor_copy(v_rep[:], v_col.broadcast_to([A, P])))
            m5 = v(lambda: V.memset(mean_w[:], 1.0 / D))
            m6 = v(lambda: V.memset(f(mod_pair[:]), 0.0))
            s0 = v(lambda: V.memset(f(sel[:]), 0.0))
            s1 = v(lambda: V.tensor_copy(sel[0:ND, :], idn[0:ND, 0:ND]), s0)
            s2 = v(lambda: V.tensor_copy(sel[32:32 + ND, :], idn[0:ND, 0:ND]), s0)
            e = a(lambda: nc.scalar.activation(alpha[:], tau[:], ACT.Exp))
            e = v(lambda: TS(alpha[:], alpha[:], 1.0, None, ALU.add), e)
            m7 = v(lambda: V.reciprocal(alpha[:], alpha[:]), e)
            t = v(lambda: V.tensor_reduce(bl_top[:], bl[:], AX, ALU.max))
            t = v(lambda: TS(bl_top[:], bl_top[:], -1.0, None, ALU.mult), t)
            for h in range(DH):
                t = a(lambda h=h: nc.scalar.activation(bl[:, h, :], bl[:, h, :], ACT.Exp, bias=bl_top[:, h:h + 1],
                                                       accum_out=bl_sum[:, h:h + 1]), t)
            t = v(lambda: V.reciprocal(bl_sum[:], bl_sum[:]), t)
            for h in range(DH):
                m8 = v(lambda h=h: TS(bl[:, h, :], bl[:, h, :], bl_sum[:, h:h + 1], 0.5, ALU.mult, ALU.mult), t)
            t = v(lambda: V.tensor_copy(typ[:, 0, :], typ_i[:]))
            t0 = v(lambda: TS(typ[:, 1, :], typ[:, 0, :], 0.0, None, ALU.is_equal), t)
            t1 = v(lambda: TS(typ[:, 2, :], typ[:, 0, :], 1.0, None, ALU.is_equal), t)
            t = v(lambda: V.tensor_tensor(typ[:, 4, :], typ[:, 1, :], typ[:, 2, :], ALU.add), t0, t1)
            t = v(lambda: TS(typ[:, 3, :], typ[:, 4, :], -1.0, 1.0, ALU.mult, ALU.add), t)
            m9 = v(lambda: TS(pen[:], typ[:, 1:4, :], NEG, None, ALU.mult), t)
            for j in range(2):
                u = v(lambda j=j: TS(cnt[:, :, j], typ[:, 1, :], jc[:, j:j + 1], None, ALU.mult), t)
                u = v(lambda j=j: V.scalar_tensor_tensor(cnt[:, :, j], typ[:, 2, :], jc[:, 2 + j:3 + j],
                                                         cnt[:, :, j], ALU.mult, ALU.add), u)
                m10 = v(lambda j=j: V.scalar_tensor_tensor(cnt[:, :, j], typ[:, 3, :], jc[:, 4:5],
                                                           cnt[:, :, j], ALU.mult, ALU.add), u)
            t = v(lambda: TS(sg[:, 1, :], sg[:, 0, :], -1.0, 1.0, ALU.mult, ALU.add))
            for e_ in range(NE):
                v(lambda e_=e_: V.tensor_tensor(coef[:, e_, :], ge[:, :, e_], sg[:, 1, :], ALU.mult), t)
            v(lambda: V.tensor_copy(coef[:, NE, :], sg[:, 0, :]))
            t = v(lambda: V.tensor_copy(ex_f[:, 0, :], ex_i[:]))
            t2 = v(lambda: TS(ex_f[:, 1, :], ex_f[:, 0, :], float(P), row_id[:], ALU.mult, ALU.add), t)
            rows = v(lambda: V.tensor_copy(ex_row[:], ex_f[:, 1, :]), t2)
            t = v(lambda: TS(onehot[:], ex_f[0:NE, 0, :], row_id[0:NE, :], None, ALU.is_equal), t)
            pe.wait(t)
            t = products(ps_side[0][:, 0:B], [(be_sb[:], onehot[:])])
            done = v(lambda: TS(bias_b[:], ps_side[0][:, 0:B], b2b, None, ALU.add), t)
            return rows, done

        rows_ready, setup_done = setup()
        act.wait(setup_done)
        pe.wait(setup_done)
        dve.wait(setup_done)
        pool.wait(setup_done)

        side_free = [setup_done, setup_done]
        turn = [0]

        def take():
            turn[0] ^= 1
            pe.wait(side_free[turn[0]])
            return turn[0]

        acc_ready, acc_stored = {}, {}
        x2_before = [None]

        def layers01(b):
            V, TS, TT, STT = nc.vector, nc.vector.tensor_scalar, nc.vector.tensor_tensor, nc.vector.scalar_tensor_tensor
            X = x_in[b % 2]
            x1, cen = temporal, ema
            for lane in (sp, pe, act, dve, pool):
                lane.wait(x2_before[0])
            if b + 1 < NBLK:
                load_x(b + 1)
            for lane in (dve, pe):
                lane.wait(x_mark[b])
            yield
            for h in range(DH):
                for s in range(BB):
                    c = slice(s * S, (s + 1) * S)
                    ctx_done = v(lambda h=h, c=c: V.tensor_tensor_scan(
                        ema[:, h, c], alpha[:, ND:ND + 1].broadcast_to([P, S]), X[:, h, c], 0.0, ALU.mult, ALU.add))
                yield
            i = take()
            m = products(ps_side[i][0:A, :], [(wn1[:, k, :], X[:, k, :]) for k in range(DH)])
            yield
            h1 = a(lambda i=i: nc.scalar.activation(small[:], ps_side[i][0:A, :], ACT.Gelu, bias=bn1), m)
            side_free[i] = h1
            for h in range(DH):
                i = take()
                m = products(ps_side[i][:], [(wsoma[:, k, h * P:(h + 1) * P], X[:, k, :]) for k in range(DH)])
                soma_done = a(lambda i=i, h=h: nc.scalar.activation(soma[:, h, :], ps_side[i][:], ACT.Gelu,
                                                                    bias=bsoma[:, h:h + 1]), m)
                side_free[i] = soma_done
                yield
            i = take()
            pe.wait(h1)
            m = products(ps_side[i][0:ND, :], [(wn2, small[:])])
            m = a(lambda i=i: nc.scalar.activation(mod[:], ps_side[i][0:ND, :], ACT.Tanh, bias=bn2_half[:],
                                                   scale=0.5), m)
            side_free[i] = m
            yield
            gate_in = [X[:, 0, :], X[:, 1, :], ema[:, 0, :], ema[:, 1, :]]
            pe.wait(ctx_done)
            for h in range(DH):
                i = take()
                g = products(ps_side[i][:], [(wg[:, k, h * P:(h + 1) * P], gate_in[k]) for k in range(4)])
                g = a(lambda i=i, h=h: nc.scalar.activation(gated[:, h, :], ps_side[i][:], ACT.Tanh,
                                                            bias=half128[:, h:h + 1], scale=0.5), g)
                side_free[i] = g
                yield
            m = v(lambda: TS(mod[:], mod[:], 0.5, 1.0, ALU.mult, ALU.add), m)
            mh = v(lambda: V.tensor_copy(mod_pair[0:ND, :], mod[:]), m)
            m = v(lambda: TT(mod_pair[32:32 + ND, :], mod[:], f(mod_pair[0:ND, :]), ALU.subtract), mh)
            gated_done = v(lambda: STT(gated[:], gated[:], 1.0, X[:], ALU.add, ALU.mult), g)
            yield

            def spread(d):
                i = take()
                pe.wait(m)
                return i, products(ps_side[i][:], [(sel[:, d:d + 1].broadcast_to([48, P]), mod_pair[:])])

            summed = [None, None]
            i_next, mb_next = spread(0)
            for d in range(ND):
                tr = trace[d % 2]
                i, mb = i_next, mb_next
                if d + 1 < ND:
                    i_next, mb_next = spread(d + 1)
                t = v(lambda i=i, tr=tr: TT(tr[:], gated[:], ps_side[i][:].unsqueeze(1).broadcast_to([P, DH, BT]),
                                            ALU.mult), mb, gated_done, summed[d % 2])
                side_free[i] = t
                yield
                for h in range(DH):
                    for s in range(BB):
                        c = slice(s * S, (s + 1) * S)
                        t2 = v(lambda h=h, c=c, d=d, tr=tr: V.tensor_tensor_scan(
                            tr[:, h, c], alpha[:, d:d + 1].broadcast_to([P, S]), tr[:, h, c], 0.0,
                            ALU.mult, ALU.add), t)
                yield
                for h in range(DH):
                    if d == 0:
                        t = v(lambda h=h, tr=tr: TS(temporal[:, h, :], tr[:, h, :], bl[:, h, 0:1], None, ALU.mult), t2)
                    else:
                        t = v(lambda h=h, d=d, tr=tr: STT(temporal[:, h, :], tr[:, h, :], bl[:, h, d:d + 1],
                                                          temporal[:, h, :], ALU.mult, ALU.add), t2, summed[(d + 1) % 2])
                summed[d % 2] = t
            yield
            prod = trace[0]
            pe.wait(summed[(ND - 1) % 2])
            for h in range(DH):
                i = take()
                g = products(ps_side[i][:], [(wtemp[:, k, h * P:(h + 1) * P], temporal[:, k, :]) for k in range(DH)])
                g = a(lambda i=i, h=h: nc.scalar.activation(prod[:, h, :], ps_side[i][:], ACT.Tanh,
                                                            bias=half128[:, 2 + h:3 + h], scale=0.5), g,
                      summed[0], summed[1])
                side_free[i] = g
                yield
            g = v(lambda: STT(prod[:], prod[:], 1.0, soma[:], ALU.add, ALU.mult), g, soma_done)
            yield
            proj = trace[1]
            pe.wait(g)
            for h in range(DH):
                i = take()
                g = products(ps_side[i][:], [(wout[:, k, h * P:(h + 1) * P], prod[:, k, :]) for k in range(DH)])
                g = a(lambda i=i, h=h: nc.scalar.activation(proj[:, h, :], ps_side[i][:], ACT.Copy, scale=0.5), g)
                side_free[i] = g
                yield
            i = take()
            pe.wait(g)
            g2 = products(ps_side[i][:], [(mean_w[:], proj[:, k, :]) for k in range(DH)])
            c_done = v(lambda i=i: TT(cen[:], proj[:], ps_side[i][:].unsqueeze(1).broadcast_to([P, DH, BT]),
                                      ALU.subtract), g2)
            side_free[i] = c_done
            yield
            g = a(lambda: nc.scalar.activation(gated[:], cen[:], ACT.Square), c_done)
            yield
            i = take()
            pe.wait(g)
            g = products(ps_side[i][:], [(mean_w[:], gated[:, k, :]) for k in range(DH)])
            g = v(lambda i=i: TS(stat[:], ps_side[i][:], 1e-5, None, ALU.add), g)
            side_free[i] = g
            yield
            g = a(lambda: nc.scalar.activation(stat[:], stat[:], ACT.Sqrt), g)
            yield
            g = v(lambda: V.reciprocal(stat[:], stat[:]), g)
            g = v(lambda: TT(cen[:], cen[:], stat[:].unsqueeze(1).broadcast_to([P, DH, BT]), ALU.mult), g)
            yield
            for h in range(DH):
                g2 = v(lambda h=h: TS(cen[:, h, :], cen[:, h, :], gamma[:, h:h + 1], beta[:, h:h + 1],
                                      ALU.mult, ALU.add), g)
            x1_done = v(lambda: TT(x1[:], cen[:], X[:], ALU.add), g2)
            yield
            i = take()
            pe.wait(x1_done)
            g = products(ps_side[i][0:A, :], [(wa1[:, k, :], x1[:, k, :]) for k in range(DH)])
            g = a(lambda i=i: nc.scalar.activation(small[:], ps_side[i][0:A, :], ACT.Tanh, bias=ba1), g)
            side_free[i] = g
            yield
            i = take()
            pe.wait(g)
            g = products(ps_side[i][:], [(v_rep[:], small[:])])
            score = [trace[0][:, s, :].rearrange("p (j l) -> p j l", j=2) for s in range(BB)]
            prob = [trace[1][:, s, :].rearrange("p (j l) -> p j l", j=2) for s in range(BB)]
            masked = []
            for s in range(BB):
                q = b * BB + s
                t = v(lambda s=s, q=q, i=i: STT(score[s], mask[:, 0], pen[:, 0, q:q + 1],
                                                ps_side[i][:, s * S:(s + 1) * S].unsqueeze(1).broadcast_to([P, 2, S]),
                                                ALU.mult, ALU.add), g)
                side_free[i] = t
                for n in (1, 2):
                    t = v(lambda s=s, q=q, n=n: STT(score[s], mask[:, n], pen[:, n, q:q + 1], score[s],
                                                    ALU.mult, ALU.add), t)
                masked.append(t)
                yield
            pooled = None
            for s in range(BB):
                q = b * BB + s
                tok = slice(s * S, (s + 1) * S)
                t = v(lambda s=s: V.tensor_reduce(top[:], score[s], AX, ALU.max), masked[s], pooled)
                t = v(lambda: TS(top[:], top[:], -1.0, None, ALU.mult), t)
                yield
                for j in range(2):
                    t2 = a(lambda s=s, j=j: nc.scalar.activation(prob[s][:, j, :], score[s][:, j, :], ACT.Exp,
                                                                 bias=top[:, j:j + 1], accum_out=den[:, j:j + 1]), t)
                i = take()
                for lh in range(2):
                    for dh in range(DH):
                        r = pe.do(lambda i=i, lh=lh, dh=dh, s=s: nc.tensor.transpose(
                            ps_side[i][:, lh * D + dh * P:lh * D + (dh + 1) * P],
                            x1[:, dh, s * S + lh * P:s * S + (lh + 1) * P], idn[:]))
                bank_i = ps_side[i][:].rearrange("p (l d) -> p l d", l=2)
                xh = a(lambda k=bank_i: nc.scalar.activation(xt_hi[:], k, ACT.Copy), r, pooled)
                xl = v(lambda k=bank_i: TT(xt_lo[:], k, f(xt_hi[:]), ALU.subtract), xh, pooled)
                side_free[i] = xl
                yield
                t = v(lambda q=q: TT(den[:], den[:], cnt[:, q, :], ALU.mult), t2)
                t = v(lambda: V.reciprocal(den[:], den[:]), t)
                for j in range(2):
                    t2 = v(lambda s=s, j=j: TS(prob[s][:, j, :], prob[s][:, j, :], den[:, j:j + 1], None, ALU.mult), t)
                yield
                i = take()
                pe.wait(t2)
                for j in range(2):
                    for lh in range(2):
                        r = pe.do(lambda i=i, lh=lh, j=j, s=s: nc.tensor.transpose(
                            ps_side[i][:, lh * S + j * P:lh * S + (j + 1) * P],
                            prob[s][:, j, lh * P:(lh + 1) * P], idn[:]))
                bank_i = ps_side[i][:].rearrange("p (l j) -> p l j", l=2)
                ph = a(lambda k=bank_i: nc.scalar.activation(pt_hi[:], k, ACT.Copy), r, pooled)
                pl = v(lambda k=bank_i: TT(pt_lo[:], k, f(pt_hi[:]), ALU.subtract), ph, pooled)
                side_free[i] = pl
                yield
                i = take()
                pe.wait(xh, xl, ph, pl)
                for dh in range(DH):
                    c = slice(dh * P, (dh + 1) * P)
                    pairs = []
                    for lh in range(2):
                        pairs += [(xt_hi[:, lh, c], pt_lo[:, lh, :]), (xt_lo[:, lh, c], pt_hi[:, lh, :]),
                                  (xt_hi[:, lh, c], pt_hi[:, lh, :])]
                    pooled = products(ps_side[i][:, dh * S:(dh + 1) * S], pairs)
                bank_i = ps_side[i][:].rearrange("p (h j) -> p h j", h=2)
                t = v(lambda k=bank_i, tok=tok: TT(acc[b % NACC][:, :, tok], k, x1[:, :, tok], ALU.add),
                      pooled, acc_stored.get(b - NACC))
                side_free[i] = t
                yield
            acc_ready[b] = t
            x2_before[0] = t

        order = [(g, e, c) for g in range(len(GROUPS)) for e in range(NE + 1) for c in range(FC)]
        w_ready, w_free = {}, {}
        raw_free = [None] * 3
        fetched, split = [0], [0]

        def fetch():
            n = fetched[0]
            if n >= len(order):
                return
            _, e, c = order[n]
            sp.wait(raw_free[n % 3])
            fetched[0] += 1
            raw_in[n] = sp.do(lambda: nc.sync.dma_start(w_raw[n % 3][:], chunks[e, c]), s_raw[n % 3], 16)

        raw_in = {}

        def split_next():
            n = split[0]
            if n >= len(order):
                return
            split[0] += 1
            k = n % WSLOTS
            act.wait(raw_in[n], w_free.get(n - WSLOTS))
            hi = act.do(lambda: nc.scalar.activation(w_hi[k][:], w_raw[n % 3][:], ACT.Copy), s_whi)
            dve.wait(hi, raw_in[n], w_free.get(n - WSLOTS))
            lo = dve.do(lambda: nc.vector.tensor_tensor(w_lo[k][:], w_raw[n % 3][:], f(w_hi[k][:]), ALU.subtract), s_wlo)
            raw_free[n % 3] = lo
            w_ready[n] = (hi, lo)
            fetch()

        hi_lo_ready, hi_lo_free = {}, [None, None]
        gu_free = [(None, None), (None, None)]
        hid_free = [None] * 3
        hl_free = [None, None]
        out_free = [setup_done]
        acc_done = {}
        step_no = [0]

        def split_x2(b, slot):
            act.wait(acc_ready[b], hi_lo_free[slot])
            dve.wait(acc_ready[b], hi_lo_free[slot])
            hi = act.do(lambda: nc.scalar.activation(x2_hi[slot][:], acc[b % NACC][:], ACT.Copy))
            dve.wait(hi)
            lo = dve.do(lambda: nc.vector.tensor_tensor(x2_lo[slot][:], acc[b % NACC][:], f(x2_hi[slot][:]), ALU.subtract))
            hi_lo_ready[b] = (hi, lo)

        class ExpertStep:

            def __init__(self, b, slot, e, c, n, last):
                self.b, self.slot, self.e, self.c, self.n, self.last = b, slot, e, c, n, last
                self.k = n % WSLOTS
                self.i = step_no[0]
                step_no[0] += 1

            def front(self):
                i, k, slot = self.i % 2, self.k, self.slot
                pe.wait(*w_ready[self.n], *hi_lo_ready[self.b], *gu_free[i])
                for out, at in ((ps_gate[i], 0), (ps_up[i], DH * P)):
                    pairs = []
                    for h in range(DH):
                        c = slice(at + h * P, at + (h + 1) * P)
                        pairs += [(w_hi[k][:, c], x2_lo[slot][:, h, :]), (w_hi[k][:, c], x2_hi[slot][:, h, :]),
                                  (w_lo[k][:, c], x2_hi[slot][:, h, :])]
                    for j, (l, r) in enumerate(pairs):
                        last = j == len(pairs) - 1
                        m = pe.do(mm(out[:], l, r, j == 0, last), s_gu, quiet=not last)
                    if at == 0:
                        self.gate = m
                self.up = m
                if self.c == FC - 1 and self.e == NE:
                    hi_lo_free[slot] = m

            def mid(self):
                i, j = self.i % 2, self.i % 3
                act.wait(self.gate, hid_free[j])
                m = act.do(lambda: nc.scalar.activation(hid[j][:], ps_gate[i][:], ACT.Silu), s_silu)
                dve.wait(m, self.up)
                self.hid = dve.do(lambda: nc.vector.tensor_tensor(hid[j][:], hid[j][:], ps_up[i][:], ALU.mult), s_hid)
                gu_free[i] = (m, self.hid)

            def late(self):
                i, j = self.i % 2, self.i % 3
                act.wait(self.hid, hl_free[i])
                self.hi = act.do(lambda: nc.scalar.activation(hid_hi[i][:], hid[j][:], ACT.Copy), s_hhi)
                pool.wait(self.hi, self.hid, hl_free[i])
                self.lo = pool.do(lambda: nc.gpsimd.tensor_tensor(hid_lo[i][:], hid[j][:], f(hid_hi[i][:]),
                                                                  ALU.subtract), s_hlo)
                hid_free[j] = self.lo

            def back(self):
                i, k = self.i % 2, self.k
                pe.wait(self.hi, self.lo)
                if self.c == 0:
                    pe.wait(out_free[0])
                at = 2 * DH * P
                for h in range(DH):
                    c = slice(at + h * P, at + (h + 1) * P)
                    triple = [(w_hi[k][:, c], hid_hi[i][:]), (w_lo[k][:, c], hid_hi[i][:]), (w_hi[k][:, c], hid_lo[i][:])]
                    for j, (l, r) in enumerate(triple):
                        last = h == DH - 1 and j == 2
                        m = pe.do(mm(ps_out[:, h, :], l, r, self.c == 0 and j == 0, self.c == FC - 1 and j == 2),
                                  s_down, quiet=not last)
                hl_free[i] = m
                if self.last:
                    w_free[self.n] = m
                if self.c == FC - 1:
                    dve.wait(m, acc_done.get(self.b), hi_lo_ready[self.b][0])
                    for s in range(BB):
                        q, tok = self.b * BB + s, slice(s * S, (s + 1) * S)
                        r = dve.do(lambda q=q, tok=tok: nc.vector.scalar_tensor_tensor(
                            acc[self.b % NACC][:, :, tok], ps_out[:, :, tok], coef[:, self.e, q:q + 1],
                            acc[self.b % NACC][:, :, tok], ALU.mult, ALU.add), s_acc)
                    out_free[0] = acc_done[self.b] = r

        we_here, we_ready, we_in_free, w2e_free = {}, {}, [None, None], [None, None]

        def gather(b):
            for s in range(BB):
                q = b * BB + s
                pool.wait(rows_ready, we_in_free[s])
                we_here[q] = pool.do(lambda q=q, s=s: nc.gpsimd.indirect_dma_start(
                    out=we_in[s][:], out_offset=None, in_=we_rows[:],
                    in_offset=bass.IndirectOffsetOnAxis(ap=ex_row[:, q:q + 1], axis=0)), s_we[s], 16)

        def route(b):
            for s in range(BB):
                act.wait(we_here[b * BB + s], w2e_free[s])
                act.do(lambda s=s: nc.scalar.activation(
                    w2e[s][:, :, PART:P], we_in[s][:].rearrange("p (c o) -> p c o", c=FC), ACT.Copy))
                m = act.do(lambda s=s: nc.scalar.activation(w2e[s][:, :, 0:PART], w2h[:, :, P:NSH], ACT.Copy))
                we_ready[b * BB + s] = we_in_free[s] = m

        class HeadStep:

            def __init__(self, b, c):
                self.b, self.c = b, c
                self.i = step_no[0]
                step_no[0] += 1

            def front(self):
                i = self.i % 2
                pe.wait(acc_done[self.b], *gu_free[i])
                for h in range(DH):
                    last = h == DH - 1
                    m = pe.do(mm(ps_gate[i][:], w1h[:, h, self.c * P:(self.c + 1) * P], acc[self.b % NACC][:, h, :],
                                 h == 0, last), s_gu, quiet=not last)
                self.pre = m

            def mid(self):
                i, j = self.i % 2, self.i % 3
                act.wait(self.pre, hid_free[j])
                self.hid = act.do(lambda: nc.scalar.activation(hid[j][:], ps_gate[i][:], ACT.Gelu,
                                                               bias=b1h[:, self.c:self.c + 1]), s_silu)
                gu_free[i] = (self.hid, gu_free[i][1])

            def late(self):
                pass

            def back(self):
                j, c = self.i % 3, self.c
                pe.wait(self.hid)
                if c == 0:
                    pe.wait(out_free[0], we_ready[self.b * BB], we_ready[self.b * BB + 1])
                pe.do(mm(ps_out[:, 0, :], w2h[:, c, 0:P], hid[j][:], c == 0, c == FC - 1), quiet=True)
                for s in range(BB):
                    tok = slice(s * S, (s + 1) * S)
                    last = s == BB - 1
                    m = pe.do(lambda s=s, tok=tok: nc.tensor.matmul(
                        ps_out[:, 1, tok], w2e[s][:, c, :], hid[j][:, tok], start=c == 0 and s == 0,
                        stop=c == FC - 1, skip_group_check=True), s_down, quiet=not last)
                hid_free[j] = m
                if c == FC - 1:
                    b = self.b
                    for s in range(BB):
                        w2e_free[s] = m
                    dve.wait(m, acc_done[b])
                    X = acc[b % NACC]
                    r = dve.do(lambda: nc.vector.scalar_tensor_tensor(X[:, 0, :], ps_out[:, 0, :], b2a, X[:, 0, :],
                                                                      ALU.add, ALU.add), s_acc)
                    for s in range(BB):
                        q, tok = b * BB + s, slice(s * S, (s + 1) * S)
                        r = dve.do(lambda q=q, tok=tok: nc.vector.scalar_tensor_tensor(
                            X[:, 1, tok], ps_out[:, 1, tok], bias_b[:, q:q + 1], X[:, 1, tok],
                            ALU.add, ALU.add), s_acc)
                    out_free[0] = r
                    sp.wait(r)
                    acc_stored[b] = sp.do(lambda: nc.sync.dma_start(y_blk[:, :, b * BT:(b + 1) * BT], X[:]),
                                          s_y[b % NACC], 16)

        for _ in range(3):
            fetch()
        for _ in layers01(0):
            pass

        pieces = 75
        side = {"made": 0, "due": 0.0, "rate": 0.0, "work": iter(())}

        def some_side_work():
            side["due"] += side["rate"]
            while side["made"] < side["due"]:
                side["made"] += 1
                if next(side["work"], "end") == "end":
                    side["rate"] = 0.0
                    return

        queue = []

        def run(step):
            step.front()
            step.mid()
            queue.append(step)
            if len(queue) > 1:
                queue[-2].late()
            if len(queue) > 2:
                queue.pop(0).back()
            some_side_work()

        def finish():
            if queue:
                queue[-1].late()
            while queue:
                queue.pop(0).back()

        def chain(blocks):
            for b in blocks:
                yield from layers01(b)

        for _ in range(WSLOTS - 1):
            split_next()
        for slot, b in enumerate(GROUPS[0]):
            split_x2(b, slot)
        for g, blocks in enumerate(GROUPS):
            ahead = GROUPS[g + 1] if g + 1 < len(GROUPS) else []
            steps = (NE + 1) * FC * len(blocks)
            side.update(made=0, due=0.0, rate=pieces * len(ahead) / (steps - 6), work=chain(ahead))
            for e in range(NE + 1):
                for slot, b in enumerate(blocks):
                    for c in range(FC):
                        n = (g * (NE + 1) + e) * FC + c
                        while split[0] <= n:
                            split_next()
                        run(ExpertStep(b, slot, e, c, n, slot == len(blocks) - 1))
                        while split[0] < len(order) and (split[0] < WSLOTS or split[0] - WSLOTS in w_free):
                            split_next()
            for _ in side["work"]:
                pass
            side["rate"] = 0.0
            for b in blocks:
                gather(b)
                if any(step.b == b for step in queue):
                    finish()
                for c in range(FC):
                    run(HeadStep(b, c))
                    if c == 1:
                        route(b)
                    if b == blocks[-1] and c == 1:
                        for slot, b2 in enumerate(ahead):
                            split_x2(b2, slot)
        finish()
        for b in range(NBLK):
            sp.wait(acc_stored[b])

        block = ctx.enter_context(nc.Block())

        @block.sync
        def _(eng):
            for w in sp.work:
                w(eng)

        @block.tensor
        def _(eng):
            for w in pe.work:
                w(eng)

        @block.vector
        def _(eng):
            for w in dve.work:
                w(eng)

        @block.scalar
        def _(eng):
            for w in act.work:
                w(eng)

        @block.gpsimd
        def _(eng):
            for w in pool.work:
                w(eng)


def kernel(**inputs):
    import numpy as np
    import concourse.bacc as bacc
    from concourse.bass_utils import run_bass_kernel_spmd

    g = {k: np.asarray(v) for k, v in inputs.items()}

    def rows(w):
        k = w.shape[0] // P
        return np.ascontiguousarray(w.reshape(k, P, -1).transpose(1, 0, 2)).reshape(P, -1)

    def cols(v):
        return v.reshape(-1, P).T

    def chunk_rows(gate, up, down):
        first = [w.reshape(DH, P, FC, P).transpose(2, 1, 0, 3).reshape(FC, P, DH * P) for w in (gate, up)]
        return np.concatenate(first + [down.reshape(FC, P, D)], axis=2)

    gs = [chunk_rows(g["L2_cond_Wg"][e], g["L2_cond_Wu"][e], g["L2_cond_Wd"][e]) for e in range(NE)]
    gs.append(chunk_rows(g["L2_cond_Sg"], g["L2_cond_Su"], g["L2_cond_Sd"]))
    f32 = np.float32
    j = np.arange(S).reshape(2, P).T
    key = np.arange(S)
    masks = np.stack([key > j[:, :, None], key < j[:, :, None], key == j[:, :, None]], 1).astype(f32)
    jcount = np.concatenate([j + 1, S - j, np.full((P, 1), S - 1)], 1).astype(f32)
    be_pad = np.zeros((NE, P), f32)
    be_pad[:, PART:] = g["L3_cond_be"]
    b2 = g["L3_cond_b2"]
    b2b = np.zeros((P,), f32)
    b2b[:PART] = b2[P:]
    arrays = {
        "xT": g["x"].reshape(T, D).T,
        "chunks": np.stack(gs),
        "sidew": np.concatenate([rows(g["L0_cond_Wg"].T), rows(g["L0_cond_Wtemp"].T), rows(g["L0_cond_Wsoma"].T),
                                 rows(g["L0_cond_Wout"].T), rows(g["L0_cond_Wn1"].T), rows(g["L1_cond_W1"])], 1),
        "vec128": np.concatenate([cols(g[n]) for n in ("L0_cond_bg", "L0_cond_bsoma", "L0_cond_btemp",
                                                       "L0_cond_gamma", "L0_cond_beta", "L3_cond_b1")]
                                 + [b2[:P, None], b2b[:, None]], 1),
        "w64": np.concatenate([g["cond_256"].T, g["L0_cond_bn1"][:, None], g["L1_cond_b1"][:, None],
                               g["L1_cond_v"][:, None]], 1),
        "vec16": g["condB_bn2"][:, None],
        "masks": masks,
        "ident": np.eye(P, dtype=f32),
        "l3w1": rows(g["L3_cond_W1"]).reshape(P, DH, F),
        "l3w2": rows(g["L3_cond_W2"]).reshape(P, FC, NSH),
        "we_rows": g["L3_cond_We"].reshape(NE, FC, P, PART).transpose(0, 2, 1, 3).reshape(NE * P, FC * PART),
        "be_pad": be_pad,
        "blendT": rows(g["cond_1024"].T).reshape(P, DH, ND),
        "taus": np.concatenate([g["condB_tauraws"], g["L0_cond_tau_ctx"].reshape(1)]),
        "types": g["itok_B_0_2"],
        "experts": g["itok_B_0_7"],
        "gates": g["fside_Bx8_0"],
        "shared_gate": g["condB_sharedgateprob"],
        "jcount": jcount,
        "prow": np.arange(P, dtype=f32)[:, None],
    }
    nc = bacc.Bacc("TRN2", target_bir_lowering=False, num_devices=1)
    maps, args = {}, []
    for name, arr in arrays.items():
        arr = np.ascontiguousarray(arr)
        maps[f"in_{name}"] = arr
        args.append(nc.dram_tensor(f"in_{name}", arr.shape, mybir.dt.from_np(arr.dtype), kind="ExternalInput").ap())
    args.append(nc.dram_tensor("out_yT", (D, T), mybir.dt.float32, kind="ExternalOutput").ap())
    residual_stack_kernel(nc, *args)
    r = run_bass_kernel_spmd(nc, [maps], core_ids=[0])
    return np.ascontiguousarray(r.results[0]["out_yT"].T).reshape(B, S, D)
```

```python
from contextlib import ExitStack

import concourse.bass as bass
from concourse import mybir

P = 128
B, S, D = 16, 256, 256
T = B * S
DH = D // P
BB = 2
BT = BB * S
NBLK = T // BT
ND = 16
NE, F = 8, 1024
FC = F // P
PART, NSH = 64, 192
A = 64
GROUPS = [[0], [1], [2, 3], [4, 5], [6, 7]]
SLOT = [0, 1, 0, 1, 0, 1, 0, 1]
WSLOTS = 9
WROW = DH * P * 2 + D
NRAW = 3
HROW = DH * P + NSH
PIECES = 42
NACC = 4
NEG = -1e30


class Counter:

    def __init__(self, sem):
        self.sem, self.count = sem, 0

    def after(self, by):
        self.count += by
        return self, self.count


class Lane:

    def __init__(self, counter):
        self.work, self.passed, self.counter = [], {}, counter

    def wait(self, *marks):
        for mark in marks:
            if mark is None:
                continue
            counter, count = mark
            if self.passed.get(counter, 0) < count:
                self.passed[counter] = count
                self.work.append(lambda eng, s=counter.sem, c=count: eng.wait_ge(s, c))

    def do(self, build, counter=None, by=1, quiet=False):
        if quiet:
            self.work.append(lambda eng: build())
            return None
        counter = counter or self.counter
        self.work.append(lambda eng: build().then_inc(counter.sem, by))
        return counter.after(by)

    def last(self):
        return self.counter, self.counter.count


def residual_stack_kernel(nc, xT, chunks, head_chunks, sidew, vec128, w64, vec16, masks, ident, we_rows,
                          be_pad, blendT, taus, types, experts, gates, shared_gate, jcount, prow, yT):
    fp32, f32r, bf16 = mybir.dt.float32, mybir.dt.float32r, mybir.dt.bfloat16
    i32, u32 = mybir.dt.int32, mybir.dt.uint32
    ALU, ACT = mybir.AluOpType, mybir.ActivationFunctionType
    AX = mybir.AxisListType.X
    ctx = ExitStack()
    with ctx:
        def sb(name, shape, dt=fp32):
            return ctx.enter_context(nc.sbuf_tensor(name, shape, dt))

        def counter(name):
            return Counter(ctx.enter_context(nc.semaphore(name)))

        w_hi = [sb(f"w_hi{i}", [P, WROW], f32r) for i in range(WSLOTS)]
        w_lo = [sb(f"w_lo{i}", [P, WROW], f32r) for i in range(WSLOTS)]
        w_raw = [sb(f"w_raw{i}", [P, WROW]) for i in range(NRAW)]
        res_hi = [sb(f"res_hi{i}", [P, DH, BT], f32r) for i in range(2)]
        res_lo = [sb(f"res_lo{i}", [P, DH, BT], f32r) for i in range(2)]
        acc = [sb(f"acc{i}", [P, DH, BT]) for i in range(NACC)]
        hid = [sb(f"hid{i}", [P, BT]) for i in range(3)]
        hid_hi = [sb(f"hid_hi{i}", [P, BT], f32r) for i in range(2)]
        hid_lo = [sb(f"hid_lo{i}", [P, BT], f32r) for i in range(2)]
        we_in = [sb(f"we_in{i}", [P, FC * PART]) for i in range(2 * BB)]
        x_in = [sb(f"x_in{i}", [P, DH, BT]) for i in range(2)]
        ema = [sb(f"ema{s}", [P, DH, S]) for s in range(BB)]
        gated = [sb(f"gated{s}", [P, DH, S]) for s in range(BB)]
        temporal = [sb(f"temporal{s}", [P, DH, S]) for s in range(BB)]
        trace = [[sb(f"trace{s}_{i}", [P, DH, S]) for i in range(3)] for s in range(BB)]
        soma = [sb(f"soma{s}", [P, DH, S]) for s in range(BB)]
        small = [sb(f"small{s}", [A, S]) for s in range(BB)]
        mod_pair = [sb(f"mod_pair{s}", [48, S], f32r) for s in range(BB)]
        stat = [sb(f"stat{s}", [P, S]) for s in range(BB)]
        one_hi = [sb(f"one_hi{s}", [P, DH, S], f32r) for s in range(BB)]
        one_lo = [sb(f"one_lo{s}", [P, DH, S], f32r) for s in range(BB)]
        two_hi = [sb(f"two_hi{s}", [P, DH, S], f32r) for s in range(BB)]
        two_lo = [sb(f"two_lo{s}", [P, DH, S], f32r) for s in range(BB)]
        top = [sb(f"top{s}", [P, 2]) for s in range(BB)]
        den = [sb(f"den{s}", [P, 2]) for s in range(BB)]
        NSPLIT = 10 * D + 2 * A
        side_hi = sb("side_hi", [P, NSPLIT], f32r)
        side_lo = sb("side_lo", [P, NSPLIT], f32r)

        def weight(at, halves, width):
            return [t[:, at:at + halves * width].rearrange("p (k e) -> p k e", k=halves) for t in (side_hi, side_lo)]

        wg, wtemp, wsoma, wout, wn1 = (weight(at, n, w) for at, n, w in (
            (0, 4, D), (4 * D, 2, D), (6 * D, 2, D), (8 * D, 2, D), (10 * D, 2, A)))
        wa1_t = sb("wa1", [P, DH, A])
        v128 = sb("v128", [P, vec128.shape[1]])
        bg, bsoma, btemp = v128[:, 0:2], v128[:, 2:4], v128[:, 4:6]
        gamma, beta, b1h, b2a = v128[:, 6:8], v128[:, 8:10], v128[:, 10:18], v128[:, 18:19]
        b2b = v128[:, 19:20]
        half128 = sb("half128", [P, 4])
        c64 = sb("c64", [A, w64.shape[1]])
        wn2, bn1, ba1, v_col = c64[:, 0:ND], c64[:, ND:ND + 1], c64[:, ND + 1:ND + 2], c64[:, ND + 2:ND + 3]
        v_rep = sb("v_rep", [A, P])
        bn2 = sb("bn2", [ND, 1])
        bn2_half = sb("bn2_half", [ND, 1])
        mask = sb("mask", [P, 3, 2, S], bf16)
        idn = sb("idn", [P, P])
        sel = sb("sel", [48, ND], f32r)
        mean_w = sb("mean_w", [P, P], f32r)
        row_sum = sb("row_sum", [P, DH])
        eps = sb("eps", [P, 1])
        bl = sb("bl", [P, DH, ND])
        bl_top = sb("bl_top", [P, DH])
        bl_sum = sb("bl_sum", [P, DH])
        tau = sb("tau", [P, ND + 1])
        alpha = sb("alpha", [P, ND + 1])
        typ_i = sb("typ_i", [P, B], i32)
        typ = sb("typ", [P, 5, B])
        pen = sb("pen", [P, 3, B])
        cnt = sb("cnt", [P, B, 2])
        jc = sb("jc", [P, 5])
        ge = sb("ge", [P, B, NE])
        sg = sb("sg", [P, 2, B])
        coef = sb("coef", [P, NE + 1, B])
        ex_i = sb("ex_i", [P, B], i32)
        ex_f = sb("ex_f", [P, 2, B])
        ex_row = sb("ex_row", [P, B], u32)
        onehot = sb("onehot", [NE, B])
        be_sb = sb("be_sb", [NE, P])
        bias_b = sb("bias_b", [P, B])
        row_id = sb("row_id", [P, 1])

        bank = [ctx.enter_context(nc.psum_tensor(f"bank{i}", [P, 512], fp32)) for i in range(6)]
        ps_gate, ps_up, ps_side = bank[0:2], bank[2:4], bank[4:6]
        ps_out = ctx.enter_context(nc.psum_tensor("ps_out", [P, DH, BT], fp32))

        pe, act, dve, pool, sp = (Lane(counter(f"{n}_side")) for n in ("pe", "act", "dve", "pool", "sp"))
        s_early, s_late, s_mask = counter("early_in"), counter("late_in"), counter("mask_in")
        s_raw = [counter(f"raw_in{i}") for i in range(NRAW)]
        s_x = [counter(f"x_in{i}") for i in range(2)]
        s_we = [counter(f"we_in{i}") for i in range(2 * BB)]
        s_y = [counter(f"y_out{i}") for i in range(NACC)]
        s_whi, s_wlo, s_rhi, s_rlo = counter("w_hi"), counter("w_lo"), counter("res_hi"), counter("res_lo")
        s_gu, s_act, s_hid = counter("gate_up"), counter("activated"), counter("hidden")
        s_hhi, s_hlo, s_down, s_acc = counter("hidden_hi"), counter("hidden_lo"), counter("down"), counter("acc")

        def f(t):
            return t.bitcast(fp32)

        V, TS, TT, STT = nc.vector, nc.vector.tensor_scalar, nc.vector.tensor_tensor, nc.vector.scalar_tensor_tensor
        activate = nc.scalar.activation

        def products(out, pairs, counter=None, start=True, stop=True, lone=True):
            for i, (l, r) in enumerate(pairs):
                last = i == len(pairs) - 1
                mark = pe.do(lambda l=l, r=r, first=i == 0, last=last: nc.tensor.matmul(
                    out, l, r, start=start and first, stop=stop and last, skip_group_check=not lone),
                    counter, quiet=not last)
            return mark

        def exact(pairs):
            out = []
            for wh, wl, xh, xl in pairs:
                out += [(wh, xl), (wl, xh), (wh, xh)]
            return out

        def v(build, *marks):
            dve.wait(*marks)
            return dve.do(build)

        def a(build, *marks):
            act.wait(*marks)
            return act.do(build)

        def split(hi, lo, src, *marks):
            h = a(lambda: activate(hi, src, ACT.Copy), *marks)
            return h, v(lambda: TT(lo, src, f(hi), ALU.subtract), h, *marks)

        x_blk = xT.rearrange("(h p) t -> p h t", p=P)
        y_blk = yT.rearrange("(h p) t -> p h t", p=P)
        x_mark = {}

        def load_x(b):
            x_mark[b] = sp.do(lambda: nc.sync.dma_start(x_in[b % 2][:], x_blk[:, :, b * BT:(b + 1) * BT]),
                              s_x[b % 2], 16)

        def load(dst, src, counter):
            return sp.do(lambda: nc.sync.dma_start(dst, src), counter, 16)

        stage = [(x_in[1], 0), (acc[1], 4 * D), (acc[2], 8 * D)]
        load_x(0)
        load(tau[:], taus.partition_broadcast(P), s_early)
        load(v128[:], vec128[:], s_early)
        load(c64[:], w64[:], s_early)
        load(bn2[:], vec16[:], s_early)
        load(idn[:], ident[:], s_early)
        load(bl[:], blendT[:], s_early)
        for t, at in stage:
            n = min(4 * D, NSPLIT - at)
            early = load(t[:].rearrange("p h t -> p (h t)")[:, 0:n], sidew[:, at:at + n], s_early)
        mask_raw = acc[3][:].rearrange("p h t -> p (h t)")
        load(wa1_t[:].rearrange("p k a -> p (k a)"), sidew[:, NSPLIT:NSPLIT + 2 * A], s_late)
        for dst, src in ((typ_i[:], types.partition_broadcast(P)), (jc[:], jcount[:]),
                         (ge[:], gates.partition_broadcast(P)), (sg[:, 0, :], shared_gate.partition_broadcast(P)),
                         (ex_i[:], experts.partition_broadcast(P)), (row_id[:], prow[:]), (be_sb[:], be_pad[:])):
            late = load(dst, src, s_late)
        mask_a = load(mask_raw, masks[:, 0:2].rearrange("p n j l -> p (n j l)"), s_mask)

        def setup_early():
            for lane in (dve, act):
                lane.wait(early)
            e = a(lambda: activate(alpha[:], tau[:], ACT.Exp))
            v(lambda: TS(half128[:, 0:2], bg, 0.5, None, ALU.mult))
            v(lambda: TS(half128[:, 2:4], btemp, 0.5, None, ALU.mult))
            v(lambda: TS(bn2_half[:], bn2[:], 0.5, None, ALU.mult))
            e = v(lambda: TS(alpha[:], alpha[:], 1.0, None, ALU.add), e)
            v(lambda: V.reciprocal(alpha[:], alpha[:]), e)
            w = acc[2][:].rearrange("p h t -> p (h t)")[:, 0:2 * D].rearrange("p (k e) -> p k e", k=2)
            t = v(lambda: V.tensor_reduce(row_sum[:], w, AX, ALU.add))
            t = v(lambda: TS(row_sum[:], row_sum[:], -1.0 / D, None, ALU.mult), t)
            for k in range(DH):
                centred = v(lambda k=k: TS(w[:, k, :], w[:, k, :], row_sum[:, k:k + 1], None, ALU.add), t)
            for t, at in stage:
                n = min(4 * D, NSPLIT - at)
                m = split(side_hi[:, at:at + n], side_lo[:, at:at + n],
                          t[:].rearrange("p h t -> p (h t)")[:, 0:n], centred if at == 8 * D else None)
            pe.wait(*m)
            t = v(lambda: V.memset(stat[0][:, 0:P], 1.0 / D))
            v(lambda: V.tensor_copy(mean_w[:], stat[0][:, 0:P]), t)
            for s in range(BB):
                v(lambda s=s: V.memset(f(mod_pair[s][:]), 0.0))
            v(lambda: V.memset(eps[:], 1e-5))
            t = v(lambda: V.memset(f(sel[:]), 0.0))
            v(lambda: V.tensor_copy(sel[0:ND, :], idn[0:ND, 0:ND]), t)
            done = v(lambda: V.tensor_copy(sel[32:32 + ND, :], idn[0:ND, 0:ND]), t)
            return m, done

        def setup_blend():
            t = v(lambda: V.tensor_reduce(bl_top[:], bl[:], AX, ALU.max))
            t = v(lambda: TS(bl_top[:], bl_top[:], -1.0, None, ALU.mult), t)
            for h in range(DH):
                t = a(lambda h=h: activate(bl[:, h, :], bl[:, h, :], ACT.Exp, bias=bl_top[:, h:h + 1],
                                           accum_out=bl_sum[:, h:h + 1]), t)
            t = v(lambda: V.reciprocal(bl_sum[:], bl_sum[:]), t)
            for h in range(DH):
                m = v(lambda h=h: TS(bl[:, h, :], bl[:, h, :], bl_sum[:, h:h + 1], 0.5, ALU.mult, ALU.mult), t)
            return m

        def setup_late():
            for lane in (dve, act, pe, pool):
                lane.wait(late, mask_a)
            v(lambda: V.tensor_copy(v_rep[:], v_col.broadcast_to([A, P])))
            v(lambda: V.tensor_copy(mask[:, 0:2].rearrange("p n j l -> p (n j l)"), mask_raw))
            v(lambda: V.memset(mask[:, 2], 0.0))
            eq = (lambda j: mask[:, 2, j, j * P:(j + 1) * P])
            t = None
            for j in range(2):
                t = v(lambda j=j: V.tensor_copy(eq(j), idn[:]), dve.last())
            t = v(lambda: V.tensor_copy(typ[:, 0, :], typ_i[:]))
            t0 = v(lambda: TS(typ[:, 1, :], typ[:, 0, :], 0.0, None, ALU.is_equal), t)
            t1 = v(lambda: TS(typ[:, 2, :], typ[:, 0, :], 1.0, None, ALU.is_equal), t)
            t = v(lambda: TT(typ[:, 4, :], typ[:, 1, :], typ[:, 2, :], ALU.add), t0, t1)
            t = v(lambda: TS(typ[:, 3, :], typ[:, 4, :], -1.0, 1.0, ALU.mult, ALU.add), t)
            v(lambda: TS(pen[:], typ[:, 1:4, :], NEG, None, ALU.mult), t)
            for j in range(2):
                u = v(lambda j=j: TS(cnt[:, :, j], typ[:, 1, :], jc[:, j:j + 1], None, ALU.mult), t)
                u = v(lambda j=j: STT(cnt[:, :, j], typ[:, 2, :], jc[:, 2 + j:3 + j], cnt[:, :, j],
                                      ALU.mult, ALU.add), u)
                v(lambda j=j: STT(cnt[:, :, j], typ[:, 3, :], jc[:, 4:5], cnt[:, :, j], ALU.mult, ALU.add), u)
            t = v(lambda: TS(sg[:, 1, :], sg[:, 0, :], -1.0, 1.0, ALU.mult, ALU.add))
            for e in range(NE):
                v(lambda e=e: TT(coef[:, e, :], ge[:, :, e], sg[:, 1, :], ALU.mult), t)
            v(lambda: V.tensor_copy(coef[:, NE, :], sg[:, 0, :]))
            t = v(lambda: V.tensor_copy(ex_f[:, 0, :], ex_i[:]))
            t2 = v(lambda: TS(ex_f[:, 1, :], ex_f[:, 0, :], float(P), row_id[:], ALU.mult, ALU.add), t)
            rows = v(lambda: V.tensor_copy(ex_row[:], ex_f[:, 1, :]), t2)
            t = v(lambda: TS(onehot[:], ex_f[0:NE, 0, :], row_id[0:NE, :], None, ALU.is_equal), t)
            pe.wait(t)
            t = products(ps_gate[0][:, 0:B], [(be_sb[:], onehot[:])])
            done = v(lambda: TS(bias_b[:], ps_gate[0][:, 0:B], b2b, None, ALU.add), t)
            return rows, done

        weights_split, early_done = setup_early()
        blend_done = setup_blend()
        pe.wait(early_done)
        act.wait(blend_done)
        late_marks = {}

        res_ready, acc_stored, side_done = {}, {}, [None, None]

        def layers01(b, s):
            q = b * BB + s
            tok = slice(s * S, (s + 1) * S)
            X = x_in[b % 2][:, :, tok]
            x1, cen, sm = temporal[s], ema[s], small[s]
            one, two = (one_hi[s], one_lo[s]), (two_hi[s], two_lo[s])
            ps = ps_side[s]
            both = ps[:].rearrange("p (h t) -> p h t", h=2)
            free = [None]

            for lane in (pe, act, dve, pool):
                lane.wait(side_done[s], x_mark[b])

            def project(w, pairs, *marks):
                pe.wait(free[0], *marks)
                for h in range(DH):
                    c = slice(h * P, (h + 1) * P)
                    m = products(both[:, h, :], exact(
                        [(w[0][:, k, c], w[1][:, k, c], xh, xl) for k, (xh, xl) in enumerate(pairs)]))
                return m

            def halves(pair):
                return [(pair[0][:, h, :], pair[1][:, h, :]) for h in range(DH)]

            def upper(pair, src, *marks):
                return a(lambda: activate(pair[0][:], src, ACT.Copy), *marks)

            def lower(pair, src, hi, *marks):
                return v(lambda: TT(pair[1][:], src, f(pair[0][:]), ALU.subtract), hi, *marks)

            x_hi = upper(one, X)
            for h in range(DH):
                ctx_done = v(lambda h=h: V.tensor_tensor_scan(
                    cen[:, h, :], alpha[:, ND:ND + 1].broadcast_to([P, S]), X[:, h, :], 0.0, ALU.mult, ALU.add),
                    early_done)
            yield
            x_lo = lower(one, X, x_hi)
            ctx_hi = upper(two, cen[:], ctx_done)
            yield
            ctx_lo = lower(two, cen[:], ctx_hi)
            pe.wait(x_hi, x_lo)
            m = products(ps[0:A, 0:S], exact([(wn1[0][:, k, :], wn1[1][:, k, :], *p)
                                              for k, p in enumerate(halves(one))]))
            h1 = free[0] = a(lambda: activate(sm[:], ps[0:A, 0:S], ACT.Gelu, bias=bn1), m)
            yield
            m = project(wsoma, halves(one))
            for h in range(DH):
                soma_done = free[0] = a(lambda h=h: activate(soma[s][:, h, :], both[:, h, :], ACT.Gelu,
                                                             bias=bsoma[:, h:h + 1]), m)
            yield
            mod = stat[s][0:ND, :]
            pe.wait(h1, free[0])
            m = products(ps[0:ND, 0:S], [(wn2, sm[:])])
            m = free[0] = a(lambda: activate(mod, ps[0:ND, 0:S], ACT.Tanh, bias=bn2_half[:], scale=0.5), m, early_done)
            yield
            g = project(wg, halves(one) + halves(two), ctx_hi, ctx_lo)
            for h in range(DH):
                g2 = free[0] = a(lambda h=h: activate(gated[s][:, h, :], both[:, h, :], ACT.Tanh,
                                                      bias=half128[:, h:h + 1], scale=0.5), g)
            m = v(lambda: TS(mod, mod, 0.5, 1.0, ALU.mult, ALU.add), m)
            mh = v(lambda: V.tensor_copy(mod_pair[s][0:ND, :], mod), m)
            m = v(lambda: TT(mod_pair[s][32:32 + ND, :], mod, f(mod_pair[s][0:ND, :]), ALU.subtract), mh)
            yield
            gated_done = v(lambda: STT(gated[s][:], gated[s][:], 1.0, X, ALU.add, ALU.mult), g2)
            scanned, weighed, added = {}, {}, {}
            for d in range(ND + 2):
                yield
                if d < ND:
                    tr = trace[s][d % 3]
                    pe.wait(free[0], m)
                    mb = products(ps[:, 0:S], [(sel[:, d:d + 1].broadcast_to([48, P]), mod_pair[s][:])])
                    t = free[0] = v(lambda tr=tr: TT(
                        tr[:], gated[s][:], ps[:, 0:S].unsqueeze(1).broadcast_to([P, DH, S]), ALU.mult),
                        mb, gated_done, added.get(d - 3))
                    for h in range(DH):
                        scanned[d] = v(lambda h=h, d=d, tr=tr: V.tensor_tensor_scan(
                            tr[:, h, :], alpha[:, d:d + 1].broadcast_to([P, S]), tr[:, h, :], 0.0,
                            ALU.mult, ALU.add), t)
                if 0 < d <= ND:
                    k = d - 1
                    tr = trace[s][k % 3]
                    dst = temporal[s] if k == 0 else tr
                    act.wait(scanned[k], blend_done)
                    for h in range(DH):
                        weighed[k] = act.do(lambda h=h, k=k, tr=tr, dst=dst: activate(
                            dst[:, h, :], tr[:, h, :], ACT.Copy, scale=bl[:, h, k:k + 1]))
                if d > 1:
                    k = d - 2
                    tr = trace[s][k % 3]
                    added[k] = weighed[k]
                    if k:
                        pool.wait(weighed[k], added[k - 1])
                        added[k] = pool.do(lambda tr=tr: nc.gpsimd.tensor_tensor(
                            temporal[s][:], temporal[s][:], tr[:], ALU.add))
            yield
            prod = trace[s][0]
            t_hi = upper(one, temporal[s][:], added[ND - 1])
            yield
            t_lo = lower(one, temporal[s][:], t_hi)
            yield
            g = project(wtemp, halves(one), t_hi, t_lo)
            for h in range(DH):
                g2 = free[0] = a(lambda h=h: activate(prod[:, h, :], both[:, h, :], ACT.Tanh,
                                                      bias=half128[:, 2 + h:3 + h], scale=0.5), g)
            yield
            g = v(lambda: STT(prod[:], prod[:], 1.0, soma[s][:], ALU.add, ALU.mult), g2, soma_done)
            yield
            p_hi = upper(two, prod[:], g)
            yield
            p_lo = lower(two, prod[:], p_hi)
            yield
            g = project(wout, halves(two), p_hi, p_lo)
            c_done = free[0] = a(lambda: activate(cen[:], both, ACT.Copy, scale=0.5), g)
            g = a(lambda: activate(gated[s][:], cen[:], ACT.Square), c_done)
            q_hi = upper(one, gated[s][:], g)
            yield
            q_lo = lower(one, gated[s][:], q_hi)
            yield
            pe.wait(free[0], q_hi, q_lo)
            g = products(ps[:, 0:S], [(mean_w[:], half[:, h, :]) for half in reversed(one) for h in range(DH)])
            g = free[0] = a(lambda: activate(stat[s][:], ps[:, 0:S], ACT.Sqrt, bias=eps[:]), g)
            yield
            g = v(lambda: V.reciprocal(stat[s][:], stat[s][:]), g)
            g = v(lambda: TT(cen[:], cen[:], stat[s][:].unsqueeze(1).broadcast_to([P, DH, S]), ALU.mult), g, c_done)
            for h in range(DH):
                g2 = v(lambda h=h: TS(cen[:, h, :], cen[:, h, :], gamma[:, h:h + 1], beta[:, h:h + 1],
                                      ALU.mult, ALU.add), g)
            x1_done = v(lambda: TT(x1[:], cen[:], X, ALU.add), g2)
            yield
            pe.wait(x1_done, free[0])
            g = products(ps[0:A, 0:S], [(wa1_t[:, k, :], x1[:, k, :]) for k in range(DH)])
            g = free[0] = a(lambda: activate(sm[:], ps[0:A, 0:S], ACT.Tanh, bias=ba1), g)
            yield
            pe.wait(g)
            g = products(ps[:, 0:S], [(v_rep[:], sm[:])])
            score, prob = trace[s][0:2]
            t = free[0] = v(lambda: STT(score[:], mask[:, 0], pen[:, 0, q:q + 1],
                                        ps[:, 0:S].unsqueeze(1).broadcast_to([P, 2, S]), ALU.mult, ALU.add), g)
            for n in (1, 2):
                t = v(lambda n=n: STT(score[:], mask[:, n], pen[:, n, q:q + 1], score[:], ALU.mult, ALU.add), t)
            t = v(lambda: V.tensor_reduce(top[s][:], score[:], AX, ALU.max), t)
            t = v(lambda: TS(top[s][:], top[s][:], -1.0, None, ALU.mult), t)
            yield
            for j in range(2):
                t2 = a(lambda j=j: activate(prob[:, j, :], score[:, j, :], ACT.Exp, bias=top[s][:, j:j + 1],
                                            accum_out=den[s][:, j:j + 1]), t)
            pe.wait(free[0])
            for lh in range(2):
                for dh in range(DH):
                    r = pe.do(lambda lh=lh, dh=dh: nc.tensor.transpose(
                        ps[:, lh * D + dh * P:lh * D + (dh + 1) * P], x1[:, dh, lh * P:(lh + 1) * P], idn[:]))
            xt_hi = upper(one, both, r)
            yield
            xt_lo = free[0] = lower(one, both, xt_hi)
            t = v(lambda: TT(den[s][:], den[s][:], cnt[:, q, :], ALU.mult), t2)
            t = v(lambda: V.reciprocal(den[s][:], den[s][:]), t)
            for j in range(2):
                t2 = v(lambda j=j: TS(prob[:, j, :], prob[:, j, :], den[s][:, j:j + 1], None, ALU.mult), t)
            yield
            pe.wait(t2, free[0])
            for j in range(2):
                for lh in range(2):
                    r = pe.do(lambda lh=lh, j=j: nc.tensor.transpose(
                        ps[:, lh * S + j * P:lh * S + (j + 1) * P], prob[:, j, lh * P:(lh + 1) * P], idn[:]))
            pt_hi = upper(two, both, r)
            yield
            pt_lo = free[0] = lower(two, both, pt_hi)
            yield
            pe.wait(xt_hi, xt_lo, pt_hi, pt_lo)
            for dh in range(DH):
                c = slice(dh * P, (dh + 1) * P)
                pooled = products(both[:, dh, :], exact([(one[0][:, lh, c], one[1][:, lh, c],
                                                          two[0][:, lh, :], two[1][:, lh, :]) for lh in range(2)]))
            t = v(lambda: TT(acc[b % NACC][:, :, tok], both, x1[:], ALU.add), pooled,
                  acc_stored[b - NACC] if b >= NACC else None)
            side_done[s] = t
            res_ready.setdefault(b, []).append(t)
            yield

        def layers01_block(b):
            if b + 1 < NBLK:
                sp.wait(side_done[0], side_done[1], *weights_split)
                load_x(b + 1)
            yield from zip(*[layers01(b, s) for s in range(BB)])

        plan = []
        for blocks in GROUPS:
            plan += [("expert", e, c) for e in range(NE + 1) for c in range(FC)]
            plan += [("head", b, c) for b in blocks for c in range(FC)]
        raw_in, raw_free, w_ready, w_free = {}, [None] * NRAW, {}, {}
        fetched, cut = [0], [0]
        we_here, we_free = {}, [None] * (2 * BB)

        def fetch():
            n = fetched[0]
            if n >= len(plan):
                return
            fetched[0] += 1
            kind, e, c = plan[n]
            sp.wait(raw_free[n % NRAW])
            dst, src = ((w_raw[n % NRAW][:], chunks[e, c]) if kind == "expert"
                        else (w_raw[n % NRAW][:, 0:HROW], head_chunks[c]))
            raw_in[n] = sp.do(lambda: nc.sync.dma_start(dst, src), s_raw[n % NRAW], 16)

        def gather(b):
            for s in range(BB):
                i, q = SLOT[b] * BB + s, b * BB + s
                pool.wait(late_marks["rows"], we_free[i])
                we_here[q] = pool.do(lambda q=q, i=i: nc.gpsimd.indirect_dma_start(
                    out=we_in[i][:], out_offset=None, in_=we_rows[:],
                    in_offset=bass.IndirectOffsetOnAxis(ap=ex_row[:, q:q + 1], axis=0)), s_we[i], 16)

        def cut_next():
            n = cut[0]
            cut[0] += 1
            k, raw = n % WSLOTS, w_raw[n % NRAW]
            kind, e, c = plan[n]
            arrived = [raw_in[n]]
            if kind == "expert":
                parts = [(slice(0, WROW), raw[:])]
            else:
                rest = raw[:, HROW - PART:HROW]
                routed = [we_in[SLOT[e] * BB + s][:, c * PART:(c + 1) * PART] for s in range(BB)]
                parts = [(slice(0, HROW), raw[:, 0:HROW]), (slice(HROW, HROW + PART), routed[0]),
                         (slice(HROW + PART, HROW + 2 * PART), rest),
                         (slice(HROW + 2 * PART, HROW + 3 * PART), routed[1])]
                arrived += [we_here[e * BB + s] for s in range(BB)]
            act.wait(w_free.get(n - WSLOTS), *arrived)
            for at, src in parts:
                hi = act.do(lambda at=at, src=src: activate(w_hi[k][:, at], src, ACT.Copy), s_whi)
            dve.wait(hi, w_free.get(n - WSLOTS), *arrived)
            for at, src in parts:
                lo = dve.do(lambda at=at, src=src: TT(w_lo[k][:, at], src, f(w_hi[k][:, at]), ALU.subtract), s_wlo)
            raw_free[n % NRAW] = lo
            if kind == "head" and c == FC - 1:
                for s in range(BB):
                    we_free[SLOT[e] * BB + s] = lo
                if e + 2 < NBLK:
                    gather(e + 2)
            w_ready[n] = (hi, lo)
            fetch()

        slot_marks, slot_free = {}, [None, None]
        gu_free = [[None, None], [None, None]]
        hid_free, hl_free, out_free = [None] * 3, [None, None], [None]
        acc_done = {}
        step_no = [0]

        def split_residual(b, slot, marks):
            act.wait(slot_free[slot], *marks)
            hi = act.do(lambda: activate(res_hi[slot][:], acc[b % NACC][:], ACT.Copy), s_rhi)
            dve.wait(hi, slot_free[slot], *marks)
            lo = dve.do(lambda: TT(res_lo[slot][:], acc[b % NACC][:], f(res_hi[slot][:]), ALU.subtract), s_rlo)
            slot_marks[slot] = (hi, lo)

        class Step:

            def __init__(self, b, slot, c, n, last):
                self.b, self.slot, self.c, self.n, self.last = b, slot, c, n, last
                self.k = n % WSLOTS
                self.i = step_no[0]
                step_no[0] += 1

            def front_products(self, out, at):
                k, slot = self.k, self.slot
                cols = [slice(at + h * P, at + (h + 1) * P) for h in range(DH)]
                return products(out[:], exact([(w_hi[k][:, cols[h]], w_lo[k][:, cols[h]],
                                                res_hi[slot][:, h, :], res_lo[slot][:, h, :]) for h in range(DH)]), s_gu)

            def late(self):
                i, j = self.i % 2, self.i % 3
                act.wait(self.hid, hl_free[i])
                self.hi = act.do(lambda: activate(hid_hi[i][:], hid[j][:], ACT.Copy), s_hhi)
                pool.wait(self.hi, self.hid, hl_free[i])
                self.lo = pool.do(lambda: nc.gpsimd.tensor_tensor(hid_lo[i][:], hid[j][:], f(hid_hi[i][:]),
                                                                  ALU.subtract), s_hlo)
                hid_free[j] = self.lo

            def back_products(self, out, weight, tok=slice(0, BT), clears=True, lone=True):
                i = self.i % 2
                return products(out, exact([(weight[0], weight[1], hid_hi[i][:, tok], hid_lo[i][:, tok])]), s_down,
                                start=self.c == 0 and clears, stop=self.c == FC - 1, lone=lone)

            def back(self):
                pe.wait(self.hi, self.lo)
                if self.c == 0:
                    pe.wait(out_free[0])
                m = self.down()
                hl_free[self.i % 2] = m
                if self.last:
                    w_free[self.n] = m
                if self.c == FC - 1:
                    dve.wait(m, acc_done.get(self.b))
                    out_free[0] = acc_done[self.b] = self.close()

        class ExpertStep(Step):
            def __init__(self, e, *args):
                super().__init__(*args)
                self.e = e

            def front(self):
                i = self.i % 2
                pe.wait(*w_ready[self.n], *slot_marks[self.slot], *gu_free[i])
                self.gate = self.front_products(ps_gate[i], 0)
                self.up = self.front_products(ps_up[i], DH * P)
                slot_free[self.slot] = self.up

            def mid(self):
                i, j = self.i % 2, self.i % 3
                act.wait(self.gate, hid_free[j])
                m = act.do(lambda: activate(hid[j][:], ps_gate[i][:], ACT.Silu), s_act)
                dve.wait(m, self.up)
                self.hid = dve.do(lambda: TT(hid[j][:], hid[j][:], ps_up[i][:], ALU.mult), s_hid)
                gu_free[i] = [m, self.hid]

            def down(self):
                for h in range(DH):
                    c = slice(2 * DH * P + h * P, 2 * DH * P + (h + 1) * P)
                    m = self.back_products(ps_out[:, h, :], (w_hi[self.k][:, c], w_lo[self.k][:, c]))
                return m

            def close(self):
                X = acc[self.b % NACC]
                dve.wait(*slot_marks[self.slot])
                for s in range(BB):
                    q, tok = self.b * BB + s, slice(s * S, (s + 1) * S)
                    r = dve.do(lambda q=q, tok=tok: STT(X[:, :, tok], ps_out[:, :, tok], coef[:, self.e, q:q + 1],
                                                        X[:, :, tok], ALU.mult, ALU.add), s_acc)
                return r

        class HeadStep(Step):
            def front(self):
                i = self.i % 2
                pe.wait(*w_ready[self.n], *slot_marks[self.slot], *gu_free[i])
                self.pre = self.front_products(ps_gate[i], 0)
                slot_free[self.slot] = self.pre

            def mid(self):
                i, j = self.i % 2, self.i % 3
                act.wait(self.pre, hid_free[j])
                self.hid = act.do(lambda: activate(hid[j][:], ps_gate[i][:], ACT.Gelu,
                                                   bias=b1h[:, self.c:self.c + 1]), s_act)
                gu_free[i][0] = self.hid

            def down(self):
                hl = (w_hi[self.k], w_lo[self.k])
                self.back_products(ps_out[:, 0, :], [t[:, DH * P:(DH + 1) * P] for t in hl])
                for s in range(BB):
                    w = [t[:, (DH + 1 + s) * P:(DH + 2 + s) * P] for t in hl]
                    tok = slice(s * S, (s + 1) * S)
                    m = self.back_products(ps_out[:, 1, tok], w, tok, clears=s == 0, lone=False)
                return m

            def close(self):
                b = self.b
                X = acc[b % NACC]
                dve.wait(*slot_marks[self.slot])
                r = dve.do(lambda: STT(X[:, 0, :], ps_out[:, 0, :], b2a, X[:, 0, :], ALU.add, ALU.add), s_acc)
                for s in range(BB):
                    q, tok = b * BB + s, slice(s * S, (s + 1) * S)
                    r = dve.do(lambda q=q, tok=tok: STT(X[:, 1, tok], ps_out[:, 1, tok], bias_b[:, q:q + 1],
                                                        X[:, 1, tok], ALU.add, ALU.add), s_acc)
                sp.wait(r)
                acc_stored[b] = sp.do(lambda: nc.sync.dma_start(y_blk[:, :, b * BT:(b + 1) * BT], X[:]),
                                      s_y[b % NACC], 16)
                return r

        for _ in range(NRAW):
            fetch()
        for i, _ in enumerate(layers01_block(0)):
            if i == 12:
                late_marks["rows"], late_marks["done"] = setup_late()
        for lane in (pe, act, dve, pool):
            lane.wait(late_marks["done"])

        queue = []
        occupant = [None, None]
        final = {}
        side_work = (p for b in range(1, NBLK) for p in layers01_block(b))
        side = {"rate": 0.0, "due": 0.0}

        def some_side_work():
            side["due"] += side["rate"]
            if side["due"] >= 1.0:
                side["due"] -= 1.0
                next(side_work, None)

        to_split = [(b, kind) for blocks in GROUPS for kind in ("x2", "x3") for b in blocks]

        def split_ready(force=False):
            while to_split:
                b, kind = to_split[0]
                slot = SLOT[b]
                if kind == "x2":
                    if occupant[slot] is not None or len(res_ready.get(b, ())) < BB:
                        return
                    occupant[slot] = b
                    split_residual(b, slot, res_ready[b])
                else:
                    if b not in final or (step_no[0] < final[b] + 2 and not force):
                        return
                    split_residual(b, slot, [acc_done[b]])
                split_kinds.add(to_split.pop(0))

        split_kinds = set()

        def run(step, kind):
            split_ready()
            if (step.b, kind) not in split_kinds:
                finish()
                split_ready(force=True)
            step.front()
            step.mid()
            if kind == "x3" and step.c == FC - 1:
                occupant[step.slot] = None
            queue.append(step)
            if len(queue) > 1:
                queue[-2].late()
            if len(queue) > 2:
                back()
            while cut[0] < len(plan) and cut[0] - WSLOTS in w_free:
                cut_next()
            some_side_work()

        def back():
            step = queue.pop(0)
            step.back()
            if isinstance(step, ExpertStep) and step.e == NE and step.c == FC - 1:
                final[step.b] = step_no[0]

        def finish():
            if queue:
                queue[-1].late()
            while queue:
                back()

        def most(g):
            best, steps = 0.0, 0
            for k in range(g, len(GROUPS) - 1):
                steps += (NE + 2) * FC * len(GROUPS[k])
                best = max(best, (PIECES * GROUPS[k + 1][-1] - made[0]) / (steps - 4 * (k - g + 1)))
            return min(1.0, best)

        made = [0]

        def counted(work):
            for p in work:
                made[0] += 1
                yield p

        side_work = counted(side_work)
        gather(0)
        gather(1)
        split_ready()
        for _ in range(WSLOTS):
            cut_next()
        n0 = 0
        for g, blocks in enumerate(GROUPS):
            side["rate"] = most(g)
            for e in range(NE + 1):
                for i, b in enumerate(blocks):
                    for c in range(FC):
                        run(ExpertStep(e, b, SLOT[b], c, n0 + e * FC + c, b == blocks[-1]), "x2")
            for i, b in enumerate(blocks):
                for c in range(FC):
                    run(HeadStep(b, SLOT[b], c, n0 + (NE + 1 + i) * FC + c, True), "x3")
            n0 += (NE + 1 + len(blocks)) * FC
            while g + 1 < len(GROUPS) and len(res_ready.get(GROUPS[g + 1][-1], ())) < BB:
                next(side_work)
        finish()
        for b in range(NBLK):
            sp.wait(acc_stored[b])

        block = ctx.enter_context(nc.Block())

        @block.sync
        def _(eng):
            for w in sp.work:
                w(eng)

        @block.tensor
        def _(eng):
            for w in pe.work:
                w(eng)

        @block.vector
        def _(eng):
            for w in dve.work:
                w(eng)

        @block.scalar
        def _(eng):
            for w in act.work:
                w(eng)

        @block.gpsimd
        def _(eng):
            for w in pool.work:
                w(eng)


def kernel(**inputs):
    import numpy as np
    import concourse.bacc as bacc
    from concourse.bass_utils import run_bass_kernel_spmd

    g = {k: np.asarray(v) for k, v in inputs.items()}

    def rows(w):
        k = w.shape[0] // P
        return np.ascontiguousarray(w.reshape(k, P, -1).transpose(1, 0, 2)).reshape(P, -1)

    def cols(v):
        return v.reshape(-1, P).T

    def chunk_rows(gate, up, down):
        first = [w.reshape(DH, P, FC, P).transpose(2, 1, 0, 3).reshape(FC, P, DH * P) for w in (gate, up)]
        return np.concatenate(first + [down.reshape(FC, P, D)], axis=2)

    gs = [chunk_rows(g["L2_cond_Wg"][e], g["L2_cond_Wu"][e], g["L2_cond_Wd"][e]) for e in range(NE)]
    gs.append(chunk_rows(g["L2_cond_Sg"], g["L2_cond_Su"], g["L2_cond_Sd"]))
    w1 = g["L3_cond_W1"].reshape(DH, P, FC, P).transpose(2, 1, 0, 3).reshape(FC, P, DH * P)
    w2 = g["L3_cond_W2"].reshape(FC, P, NSH)
    head = np.concatenate([w1, w2], axis=2)
    f32 = np.float32
    j = np.arange(S).reshape(2, P).T
    key = np.arange(S)
    masks = np.stack([key > j[:, :, None], key < j[:, :, None]], 1).astype(f32)
    jcount = np.concatenate([j + 1, S - j, np.full((P, 1), S - 1)], 1).astype(f32)
    be_pad = np.zeros((NE, P), f32)
    be_pad[:, PART:] = g["L3_cond_be"]
    b2 = g["L3_cond_b2"]
    b2b = np.zeros((P,), f32)
    b2b[:PART] = b2[P:]
    arrays = {
        "xT": g["x"].reshape(T, D).T,
        "chunks": np.stack(gs),
        "head_chunks": head,
        "sidew": np.concatenate([rows(g["L0_cond_Wg"].T), rows(g["L0_cond_Wtemp"].T), rows(g["L0_cond_Wsoma"].T),
                                 rows(g["L0_cond_Wout"].T), rows(g["L0_cond_Wn1"].T), rows(g["L1_cond_W1"])], 1),
        "vec128": np.concatenate([cols(g[n]) for n in ("L0_cond_bg", "L0_cond_bsoma", "L0_cond_btemp",
                                                       "L0_cond_gamma", "L0_cond_beta", "L3_cond_b1")]
                                 + [b2[:P, None], b2b[:, None]], 1),
        "w64": np.concatenate([g["cond_256"].T, g["L0_cond_bn1"][:, None], g["L1_cond_b1"][:, None],
                               g["L1_cond_v"][:, None]], 1),
        "vec16": g["condB_bn2"][:, None],
        "masks": masks,
        "ident": np.eye(P, dtype=f32),
        "we_rows": g["L3_cond_We"].reshape(NE, FC, P, PART).transpose(0, 2, 1, 3).reshape(NE * P, FC * PART),
        "be_pad": be_pad,
        "blendT": rows(g["cond_1024"].T).reshape(P, DH, ND),
        "taus": np.concatenate([g["condB_tauraws"], g["L0_cond_tau_ctx"].reshape(1)]),
        "types": g["itok_B_0_2"],
        "experts": g["itok_B_0_7"],
        "gates": g["fside_Bx8_0"],
        "shared_gate": g["condB_sharedgateprob"],
        "jcount": jcount,
        "prow": np.arange(P, dtype=f32)[:, None],
    }
    nc = bacc.Bacc("TRN2", target_bir_lowering=False, num_devices=1)
    maps, args = {}, []
    for name, arr in arrays.items():
        arr = np.ascontiguousarray(arr)
        maps[f"in_{name}"] = arr
        args.append(nc.dram_tensor(f"in_{name}", arr.shape, mybir.dt.from_np(arr.dtype), kind="ExternalInput").ap())
    args.append(nc.dram_tensor("out_yT", (D, T), mybir.dt.float32, kind="ExternalOutput").ap())
    residual_stack_kernel(nc, *args)
    r = run_bass_kernel_spmd(nc, [maps], core_ids=[0])
    return np.ascontiguousarray(r.results[0]["out_yT"].T).reshape(B, S, D)
```

```python
from contextlib import ExitStack

import concourse.bass as bass
from concourse import mybir

P = 128
B, S, D = 16, 256, 256
T = B * S
DH = D // P
BB = 2
BT = BB * S
NBLK = T // BT
ND = 16
NE, F = 8, 1024
FC = F // P
PART, NSH = 64, 192
A = 64
HEAD = NE + 1
JOIN = [0, 9, 16, 20, 26, 30, 36, 40]
RUNS = []
for k in range(JOIN[-1] + NE + 2):
    under_way = [b for b in range(NBLK) if JOIN[b] <= k <= JOIN[b] + NE]
    if under_way:
        RUNS.append((k % (NE + 1), under_way))
    RUNS += [(HEAD, [b]) for b in range(NBLK) if k == JOIN[b] + NE + 1]
SLOT = [b % 2 for b in range(NBLK)]
WSLOTS = 9
WROW = DH * P * 2 + D
NRAW = 3
HROW = DH * P + NSH
FIRST_CUT = 23
BEHIND = 20
PIECES = 47
DEPTH = 3
NACC = 4
NEG = -1e30


class Counter:

    def __init__(self, sem):
        self.sem, self.count = sem, 0

    def after(self, by):
        self.count += by
        return self, self.count


class Lane:

    def __init__(self, counter):
        self.work, self.passed, self.counter = [], {}, counter

    def wait(self, *marks):
        for mark in marks:
            if mark is None:
                continue
            counter, count = mark
            if self.passed.get(counter, 0) < count:
                self.passed[counter] = count
                self.work.append(lambda eng, s=counter.sem, c=count: eng.wait_ge(s, c))

    def do(self, build, counter=None, by=1, quiet=False):
        if quiet:
            self.work.append(lambda eng: build())
            return None
        counter = counter or self.counter
        self.work.append(lambda eng: build().then_inc(counter.sem, by))
        return counter.after(by)

    def last(self):
        return self.counter, self.counter.count


def residual_stack_kernel(nc, xT, chunks, head_chunks, sidew, vec128, w64, vec16, masks, ident, we_rows,
                          be_pad, blendT, taus, types, experts, gates, shared_gate, jcount, prow, yT):
    fp32, f32r, bf16 = mybir.dt.float32, mybir.dt.float32r, mybir.dt.bfloat16
    i32, u32 = mybir.dt.int32, mybir.dt.uint32
    ALU, ACT = mybir.AluOpType, mybir.ActivationFunctionType
    AX = mybir.AxisListType.X
    ctx = ExitStack()
    with ctx:
        def sb(name, shape, dt=fp32):
            return ctx.enter_context(nc.sbuf_tensor(name, shape, dt))

        def counter(name):
            return Counter(ctx.enter_context(nc.semaphore(name)))

        w_hi = [sb(f"w_hi{i}", [P, WROW], f32r) for i in range(WSLOTS)]
        w_lo = [sb(f"w_lo{i}", [P, WROW], f32r) for i in range(WSLOTS)]
        w_raw = [sb(f"w_raw{i}", [P, WROW]) for i in range(NRAW)]
        res_hi = [sb(f"res_hi{i}", [P, DH, BT], f32r) for i in range(2)]
        res_lo = [sb(f"res_lo{i}", [P, DH, BT], f32r) for i in range(2)]
        acc = [sb(f"acc{i}", [P, DH, BT]) for i in range(NACC)]
        hid = [sb(f"hid{i}", [P, BT]) for i in range(3)]
        hid_hi = [sb(f"hid_hi{i}", [P, BT], f32r) for i in range(DEPTH)]
        hid_lo = [sb(f"hid_lo{i}", [P, BT], f32r) for i in range(DEPTH)]
        we_in = [sb(f"we_in{i}", [P, FC * PART]) for i in range(2 * BB)]
        x_in = [[sb(f"x_in{s}_{i}", [P, DH, S]) for i in range(2)] for s in range(BB)]
        ema = [sb(f"ema{s}", [P, DH, S]) for s in range(BB)]
        gated = [sb(f"gated{s}", [P, DH, S]) for s in range(BB)]
        temporal = [sb(f"temporal{s}", [P, DH, S]) for s in range(BB)]
        trace = [[sb(f"trace{s}_{i}", [P, DH, S]) for i in range(3)] for s in range(BB)]
        soma = [sb(f"soma{s}", [P, DH, S]) for s in range(BB)]
        small = [sb(f"small{s}", [A, S]) for s in range(BB)]
        mod_pair = [sb(f"mod_pair{s}", [48, S], f32r) for s in range(BB)]
        stat = [sb(f"stat{s}", [P, S]) for s in range(BB)]
        one_hi = [sb(f"one_hi{s}", [P, DH, S], f32r) for s in range(BB)]
        one_lo = [sb(f"one_lo{s}", [P, DH, S], f32r) for s in range(BB)]
        two_hi = [sb(f"two_hi{s}", [P, DH, S], f32r) for s in range(BB)]
        two_lo = [sb(f"two_lo{s}", [P, DH, S], f32r) for s in range(BB)]
        top = [sb(f"top{s}", [P, 2]) for s in range(BB)]
        den = [sb(f"den{s}", [P, 2]) for s in range(BB)]
        NSPLIT = 10 * D + 2 * A
        side_hi = sb("side_hi", [P, NSPLIT], f32r)
        side_lo = sb("side_lo", [P, NSPLIT], f32r)

        def weight(at, halves, width):
            staged = acc[at // (4 * D)][:].rearrange("p h t -> p (h t)")
            plain = staged[:, at % (4 * D):at % (4 * D) + halves * width]
            return [t.rearrange("p (k e) -> p k e", k=halves) for t in (
                side_hi[:, at:at + halves * width], side_lo[:, at:at + halves * width], plain)]

        wg, wtemp, wsoma, wout, wn1 = (weight(at, n, w) for at, n, w in (
            (0, 4, D), (4 * D, 2, D), (6 * D, 2, D), (8 * D, 2, D), (10 * D, 2, A)))
        wa1_t = sb("wa1", [P, DH, A])
        v128 = sb("v128", [P, vec128.shape[1]])
        bg, bsoma, btemp = v128[:, 0:2], v128[:, 2:4], v128[:, 4:6]
        gamma, beta, b1h, b2a = v128[:, 6:8], v128[:, 8:10], v128[:, 10:18], v128[:, 18:19]
        b2b = v128[:, 19:20]
        half128 = sb("half128", [P, 4])
        c64 = sb("c64", [A, w64.shape[1]])
        wn2, bn1, ba1, v_col = c64[:, 0:ND], c64[:, ND:ND + 1], c64[:, ND + 1:ND + 2], c64[:, ND + 2:ND + 3]
        bn2 = sb("bn2", [ND, 1])
        bn2_half = sb("bn2_half", [ND, 1])
        mask = sb("mask", [P, 2, 2, S], bf16)
        idn = sb("idn", [P, P])
        sel = sb("sel", [48, ND], f32r)
        mean_w = sb("mean_w", [P, P], f32r)
        row_sum = sb("row_sum", [P, DH])
        eps = sb("eps", [P, 1])
        bl = sb("bl", [P, DH, ND])
        bl_top = sb("bl_top", [P, DH])
        bl_sum = sb("bl_sum", [P, DH])
        tau = sb("tau", [P, ND + 1])
        alpha = sb("alpha", [P, ND + 1])
        typ_i = sb("typ_i", [P, B], i32)
        typ = sb("typ", [P, 5, B])
        pen = sb("pen", [P, 3, B])
        cnt = sb("cnt", [P, B, 2])
        jc = sb("jc", [P, 5])
        ge = sb("ge", [P, B, NE])
        sg = sb("sg", [P, 2, B])
        coef = sb("coef", [P, NE + 1, B])
        ex_i = sb("ex_i", [P, B], i32)
        ex_f = sb("ex_f", [P, 2, B])
        ex_row = sb("ex_row", [P, B], u32)
        onehot = sb("onehot", [NE, B])
        be_sb = sb("be_sb", [NE, P])
        bias_b = sb("bias_b", [P, B])
        row_id = sb("row_id", [P, 1])

        bank = [ctx.enter_context(nc.psum_tensor(f"bank{i}", [P, 512], fp32)) for i in range(6)]
        ps_gate, ps_up, ps_side = bank[0:2], bank[2:4], bank[4:6]
        ps_out = ctx.enter_context(nc.psum_tensor("ps_out", [P, DH, BT], fp32))

        pe, act, dve, pool, sp = (Lane(counter(f"{n}_side")) for n in ("pe", "act", "dve", "pool", "sp"))
        s_tau, s_early, s_late = counter("tau_in"), counter("early_in"), counter("late_in")
        s_side = [counter(f"side_in{i}") for i in range(3)]
        s_raw = [counter(f"raw_in{i}") for i in range(NRAW)]
        s_x = [[counter(f"x_in{s}_{i}") for i in range(2)] for s in range(BB)]
        s_we = [counter(f"we_in{i}") for i in range(2 * BB)]
        s_y = [counter(f"y_out{i}") for i in range(NACC)]
        s_whi, s_wlo, s_rhi, s_rlo = counter("w_hi"), counter("w_lo"), counter("res_hi"), counter("res_lo")
        s_gu, s_act, s_hid = counter("gate_up"), counter("activated"), counter("hidden")
        s_hhi, s_hlo, s_down, s_acc = counter("hidden_hi"), counter("hidden_lo"), counter("down"), counter("acc")

        def f(t):
            return t.bitcast(fp32)

        V, TS, TT, STT = nc.vector, nc.vector.tensor_scalar, nc.vector.tensor_tensor, nc.vector.scalar_tensor_tensor
        activate = nc.scalar.activation

        def products(out, pairs, counter=None, start=True, stop=True, lone=True):
            for i, (l, r) in enumerate(pairs):
                last = i == len(pairs) - 1
                mark = pe.do(lambda l=l, r=r, first=i == 0, last=last: nc.tensor.matmul(
                    out, l, r, start=start and first, stop=stop and last, skip_group_check=not lone),
                    counter, quiet=not last)
            return mark

        def exact(pairs):
            out = []
            for wh, wl, xh, xl in pairs:
                out += [(wh, xl), (wl, xh), (wh, xh)]
            return out

        def v(build, *marks):
            dve.wait(*marks)
            return dve.do(build)

        def a(build, *marks):
            act.wait(*marks)
            return act.do(build)

        def split(hi, lo, src, *marks):
            h = a(lambda: activate(hi, src, ACT.Copy), *marks)
            return h, v(lambda: TT(lo, src, f(hi), ALU.subtract), h, *marks)

        x_blk = xT.rearrange("(h p) t -> p h t", p=P)
        y_blk = yT.rearrange("(h p) t -> p h t", p=P)
        x_mark = {}

        def load_x(b, s):
            at = (b * BB + s) * S
            x_mark[b, s] = sp.do(lambda: nc.sync.dma_start(x_in[s][b % 2][:], x_blk[:, :, at:at + S]),
                                 s_x[s][b % 2], 16)

        def load(dst, src, counter):
            return sp.do(lambda: nc.sync.dma_start(dst, src), counter, 16)

        stage = [(acc[0], 0), (acc[1], 4 * D), (acc[2], 8 * D)]
        stage = [(t[:].rearrange("p h t -> p (h t)")[:, 0:min(4 * D, NSPLIT - at)], at) for t, at in stage]
        load_x(0, 0)
        taus_in = load(tau[:], taus.partition_broadcast(P), s_tau)
        load_x(0, 1)
        side_in = {at: load(t, sidew[:, at:at + t.shape[1]], s_side[n]) for n, (t, at) in
                   reversed(list(enumerate(stage)))}
        load(c64[:], w64[:], s_early)
        load(v128[:], vec128[:], s_early)
        load(bn2[:], vec16[:], s_early)
        load(idn[:], ident[:], s_early)
        early = load(bl[:], blendT[:], s_early)
        mask_raw = acc[3][:].rearrange("p h t -> p (h t)")
        late_loads = [(wa1_t[:].rearrange("p k a -> p (k a)"), sidew[:, NSPLIT:NSPLIT + 2 * A]),
                      (typ_i[:], types.partition_broadcast(P)), (jc[:], jcount[:]),
                      (ge[:], gates.partition_broadcast(P)), (sg[:, 0, :], shared_gate.partition_broadcast(P)),
                      (ex_i[:], experts.partition_broadcast(P)), (row_id[:], prow[:]), (be_sb[:], be_pad[:]),
                      (mask_raw, masks.rearrange("p n j l -> p (n j l)"))]

        for dst, src in late_loads:
            late = load(dst, src, s_late)

        def setup_early():
            e = a(lambda: activate(alpha[:], tau[:], ACT.Exp), taus_in)
            for s in range(BB):
                v(lambda s=s: V.memset(f(mod_pair[s][:]), 0.0))
            v(lambda: V.memset(eps[:], 1e-5))
            t2 = v(lambda: V.memset(stat[0][:, 0:P], 1.0 / D))
            t = v(lambda: V.memset(f(sel[:]), 0.0))
            e = v(lambda: TS(alpha[:], alpha[:], 1.0, None, ALU.add), e)
            alpha_done = v(lambda: V.reciprocal(alpha[:], alpha[:]), e)
            yield alpha_done
            v(lambda: V.tensor_copy(mean_w[:], stat[0][:, 0:P]), t2)
            w = stage[2][0][:, 0:2 * D].rearrange("p (k e) -> p k e", k=2)
            t2 = v(lambda: V.tensor_reduce(row_sum[:], w, AX, ALU.add), side_in[8 * D])
            t2 = v(lambda: TS(row_sum[:], row_sum[:], -1.0 / D, None, ALU.mult), t2)
            for k in range(DH):
                centred = v(lambda k=k: TS(w[:, k, :], w[:, k, :], row_sum[:, k:k + 1], None, ALU.add), t2)
            yield centred
            dve.wait(early)
            v(lambda: TS(half128[:, 0:2], bg, 0.5, None, ALU.mult))
            v(lambda: TS(half128[:, 2:4], btemp, 0.5, None, ALU.mult))
            v(lambda: TS(bn2_half[:], bn2[:], 0.5, None, ALU.mult))
            v(lambda: V.tensor_copy(sel[0:ND, :], idn[0:ND, 0:ND]), t)
            yield v(lambda: V.tensor_copy(sel[32:32 + ND, :], idn[0:ND, 0:ND]), t)

        def split_side():
            for src, at in reversed(stage):
                yield split(side_hi[:, at:at + src.shape[1]], side_lo[:, at:at + src.shape[1]], src,
                            side_in[at], dve.last())

        def setup_blend():
            t = v(lambda: V.tensor_reduce(bl_top[:], bl[:], AX, ALU.max))
            t = v(lambda: TS(bl_top[:], bl_top[:], -1.0, None, ALU.mult), t)
            for h in range(DH):
                t = a(lambda h=h: activate(bl[:, h, :], bl[:, h, :], ACT.Exp, bias=bl_top[:, h:h + 1],
                                           accum_out=bl_sum[:, h:h + 1]), t)
            t = v(lambda: V.reciprocal(bl_sum[:], bl_sum[:]), t)
            for h in range(DH):
                m = v(lambda h=h: TS(bl[:, h, :], bl[:, h, :], bl_sum[:, h:h + 1], 0.5, ALU.mult, ALU.mult), t)
            return m

        def setup_late():
            for lane in (dve, act, pe, pool):
                lane.wait(late)
            v(lambda: V.tensor_copy(mask[:].rearrange("p n j l -> p (n j l)"), mask_raw))
            t = v(lambda: V.tensor_copy(typ[:, 0, :], typ_i[:]))
            t0 = v(lambda: TS(typ[:, 1, :], typ[:, 0, :], 0.0, None, ALU.is_equal), t)
            t1 = v(lambda: TS(typ[:, 2, :], typ[:, 0, :], 1.0, None, ALU.is_equal), t)
            t = v(lambda: TT(typ[:, 4, :], typ[:, 1, :], typ[:, 2, :], ALU.add), t0, t1)
            t = v(lambda: TS(typ[:, 3, :], typ[:, 4, :], -1.0, 1.0, ALU.mult, ALU.add), t)
            v(lambda: TS(pen[:], typ[:, 1:4, :], NEG, None, ALU.mult), t)
            for j in range(2):
                u = v(lambda j=j: TS(cnt[:, :, j], typ[:, 1, :], jc[:, j:j + 1], None, ALU.mult), t)
                u = v(lambda j=j: STT(cnt[:, :, j], typ[:, 2, :], jc[:, 2 + j:3 + j], cnt[:, :, j],
                                      ALU.mult, ALU.add), u)
                v(lambda j=j: STT(cnt[:, :, j], typ[:, 3, :], jc[:, 4:5], cnt[:, :, j], ALU.mult, ALU.add), u)
            t = v(lambda: TS(sg[:, 1, :], sg[:, 0, :], -1.0, 1.0, ALU.mult, ALU.add))
            for e in range(NE):
                v(lambda e=e: TT(coef[:, e, :], ge[:, :, e], sg[:, 1, :], ALU.mult), t)
            v(lambda: V.tensor_copy(coef[:, NE, :], sg[:, 0, :]))
            t = v(lambda: V.tensor_copy(ex_f[:, 0, :], ex_i[:]))
            t2 = v(lambda: TS(ex_f[:, 1, :], ex_f[:, 0, :], float(P), row_id[:], ALU.mult, ALU.add), t)
            rows = v(lambda: V.tensor_copy(ex_row[:], ex_f[:, 1, :]), t2)
            t = v(lambda: TS(onehot[:], ex_f[0:NE, 0, :], row_id[0:NE, :], None, ALU.is_equal), t)
            yield rows
            pe.wait(t)
            t = products(ps_gate[0][:, 0:B], [(be_sb[:], onehot[:])])
            done = v(lambda: TS(bias_b[:], ps_gate[0][:, 0:B], b2b, None, ALU.add), t)
            yield done

        setting_up, splitting = setup_early(), split_side()
        alpha_done = next(setting_up)
        ready = {}
        late_marks = {}

        res_ready, acc_stored, side_done = {}, {}, [None, None]

        def layers01(b, s):
            q = b * BB + s
            tok = slice(s * S, (s + 1) * S)
            X = x_in[s][b % 2][:]
            x1, cen, sm = temporal[s], ema[s], small[s]
            plain = b == 0
            one, two = (one_hi[s], one_lo[s]), (two_hi[s], two_lo[s])
            ps = ps_side[s]
            both = ps[:].rearrange("p (h t) -> p h t", h=2)
            free = [None]

            for lane in (pe, act, dve, pool):
                lane.wait(side_done[s], x_mark[b, s])
            if b + 1 < NBLK:
                sp.wait(side_done[s])
                load_x(b + 1, s)

            def project(w, pairs, *marks):
                pe.wait(free[0], *marks)
                for h in range(DH):
                    c = slice(h * P, (h + 1) * P)
                    m = products(both[:, h, :], passes([[t[:, k, c] for t in w] for k in range(len(pairs))], pairs))
                return m

            def passes(w, pairs):
                if plain:
                    return [(t[2], x[0]) for t, x in zip(w, pairs)]
                return exact([(t[0], t[1], *x) for t, x in zip(w, pairs)])

            def halves(pair):
                return [(pair[0][:, h, :], pair[1][:, h, :]) for h in range(DH)]

            def upper(pair, src, *marks):
                if plain:
                    return marks[0] if marks else None
                return a(lambda: activate(pair[0][:], src, ACT.Copy), *marks)

            def lower(pair, src, hi, *marks):
                if plain:
                    return hi
                return v(lambda: TT(pair[1][:], src, f(pair[0][:]), ALU.subtract), hi, *marks)

            x_hi = upper(one, X)
            for h in range(DH):
                ctx_done = v(lambda h=h: V.tensor_tensor_scan(
                    cen[:, h, :], alpha[:, ND:ND + 1].broadcast_to([P, S]), X[:, h, :], 0.0, ALU.mult, ALU.add),
                    alpha_done)
            yield
            x_lo = lower(one, X, x_hi)
            ctx_hi = upper(two, cen[:], ctx_done)
            yield
            ctx_lo = lower(two, cen[:], ctx_hi)
            pe.wait(x_hi, x_lo, *ready[8])
            act.wait(early)
            xs = halves((X, X) if plain else one)
            m = products(ps[0:A, 0:S], passes([[t[:, k, :] for t in wn1] for k in range(DH)], xs))
            h1 = free[0] = a(lambda: activate(sm[:], ps[0:A, 0:S], ACT.Gelu, bias=bn1), m)
            yield
            m = project(wsoma, xs, *ready[4])
            for h in range(DH):
                soma_done = free[0] = a(lambda h=h: activate(soma[s][:, h, :], both[:, h, :], ACT.Gelu,
                                                             bias=bsoma[:, h:h + 1]), m)
            yield
            mod = stat[s][0:ND, :]
            pe.wait(h1, free[0], early)
            m = products(ps[0:ND, 0:S], [(wn2, sm[:])])
            m = free[0] = a(lambda: activate(mod, ps[0:ND, 0:S], ACT.Tanh, bias=bn2_half[:], scale=0.5), m, ready["small"])
            yield
            g = project(wg, xs + halves((cen, cen) if plain else two), ctx_hi, ctx_lo, *ready[0])
            for h in range(DH):
                g2 = free[0] = a(lambda h=h: activate(gated[s][:, h, :], both[:, h, :], ACT.Tanh,
                                                      bias=half128[:, h:h + 1], scale=0.5), g)
            m = v(lambda: TS(mod, mod, 0.5, 1.0, ALU.mult, ALU.add), m)
            mh = v(lambda: V.tensor_copy(mod_pair[s][0:ND, :], mod), m)
            m = v(lambda: TT(mod_pair[s][32:32 + ND, :], mod, f(mod_pair[s][0:ND, :]), ALU.subtract), mh)
            yield
            gated_done = v(lambda: STT(gated[s][:], gated[s][:], 1.0, X, ALU.add, ALU.mult), g2)
            scanned, weighed, added = {}, {}, {}
            for d in range(ND + 2):
                yield
                if d < ND:
                    tr = trace[s][d % 3]
                    pe.wait(free[0], m, ready["small"])
                    mb = products(ps[:, 0:S], [(sel[:, d:d + 1].broadcast_to([48, P]), mod_pair[s][:])])
                    t = free[0] = v(lambda tr=tr: TT(
                        tr[:], gated[s][:], ps[:, 0:S].unsqueeze(1).broadcast_to([P, DH, S]), ALU.mult),
                        mb, gated_done, added.get(d - 3))
                    for h in range(DH):
                        scanned[d] = v(lambda h=h, d=d, tr=tr: V.tensor_tensor_scan(
                            tr[:, h, :], alpha[:, d:d + 1].broadcast_to([P, S]), tr[:, h, :], 0.0,
                            ALU.mult, ALU.add), t)
                if 0 < d <= ND:
                    k = d - 1
                    tr = trace[s][k % 3]
                    dst = temporal[s] if k == 0 else tr
                    act.wait(scanned[k], ready["blend"])
                    for h in range(DH):
                        weighed[k] = act.do(lambda h=h, k=k, tr=tr, dst=dst: activate(
                            dst[:, h, :], tr[:, h, :], ACT.Copy, scale=bl[:, h, k:k + 1]))
                if d > 1:
                    k = d - 2
                    tr = trace[s][k % 3]
                    added[k] = weighed[k]
                    if k:
                        pool.wait(weighed[k], added[k - 1])
                        added[k] = pool.do(lambda tr=tr: nc.gpsimd.tensor_tensor(
                            temporal[s][:], temporal[s][:], tr[:], ALU.add))
            yield
            prod = trace[s][0]
            t_hi = upper(one, temporal[s][:], added[ND - 1])
            yield
            t_lo = lower(one, temporal[s][:], t_hi)
            yield
            g = project(wtemp, halves((temporal[s], temporal[s]) if plain else one), t_hi, t_lo)
            for h in range(DH):
                g2 = free[0] = a(lambda h=h: activate(prod[:, h, :], both[:, h, :], ACT.Tanh,
                                                      bias=half128[:, 2 + h:3 + h], scale=0.5), g)
            yield
            g = v(lambda: STT(prod[:], prod[:], 1.0, soma[s][:], ALU.add, ALU.mult), g2, soma_done)
            yield
            p_hi = upper(two, prod[:], g)
            yield
            p_lo = lower(two, prod[:], p_hi)
            yield
            g = project(wout, halves((prod, prod) if plain else two), p_hi, p_lo)
            c_done = free[0] = a(lambda: activate(cen[:], both, ACT.Copy, scale=0.5), g)
            squared = a(lambda: activate(gated[s][:], cen[:], ACT.Square), c_done)
            g = squared
            q_hi = upper(one, gated[s][:], g)
            yield
            q_lo = lower(one, gated[s][:], q_hi)
            yield
            pe.wait(free[0], q_hi, q_lo)
            g = products(ps[:, 0:S], [(mean_w[:] if not plain else f(mean_w[:]), half[:, h, :])
                                      for half in ([gated[s]] if plain else reversed(one)) for h in range(DH)])
            g = free[0] = a(lambda: activate(stat[s][:], ps[:, 0:S], ACT.Sqrt, bias=eps[:]), g)
            yield
            g = v(lambda: V.reciprocal(stat[s][:], stat[s][:]), g)
            if not plain:
                yield
            g = v(lambda: TT(cen[:], cen[:], stat[s][:].unsqueeze(1).broadcast_to([P, DH, S]), ALU.mult), g, c_done)
            yield
            for h in range(DH):
                g2 = v(lambda h=h: TS(cen[:, h, :], cen[:, h, :], gamma[:, h:h + 1], beta[:, h:h + 1],
                                      ALU.mult, ALU.add), g)
            x1_done = v(lambda: TT(x1[:], cen[:], X, ALU.add), g2)
            yield
            if not plain:
                yield
            pe.wait(x1_done, free[0])
            g = products(ps[0:A, 0:S], [(wa1_t[:, k, :], x1[:, k, :]) for k in range(DH)])
            g = free[0] = a(lambda: activate(sm[:], ps[0:A, 0:S], ACT.Tanh, bias=ba1), g)
            yield
            pe.wait(g)
            g = products(ps[:, 0:S], [(v_col.broadcast_to([A, P]), sm[:])])
            score, prob = trace[s][0:2]
            t = free[0] = v(lambda: STT(score[:], mask[:, 0], pen[:, 0, q:q + 1],
                                        ps[:, 0:S].unsqueeze(1).broadcast_to([P, 2, S]), ALU.mult, ALU.add), g)
            t = v(lambda: STT(score[:], mask[:, 1], pen[:, 1, q:q + 1], score[:], ALU.mult, ALU.add), t)
            for j in range(2):
                at = score[:, j, j * P:(j + 1) * P]
                t2 = v(lambda at=at: STT(at, idn[:], pen[:, 2, q:q + 1], at, ALU.mult, ALU.add), t)
            t = t2
            yield
            t = v(lambda: V.tensor_reduce(top[s][:], score[:], AX, ALU.max), t)
            t = v(lambda: TS(top[s][:], top[s][:], -1.0, None, ALU.mult), t)
            yield
            for j in range(2):
                t2 = a(lambda j=j: activate(prob[:, j, :], score[:, j, :], ACT.Exp, bias=top[s][:, j:j + 1],
                                            accum_out=den[s][:, j:j + 1]), t)
            pe.wait(free[0])
            for lh in range(2):
                for dh in range(DH):
                    r = pe.do(lambda lh=lh, dh=dh: nc.tensor.transpose(
                        ps[:, lh * D + dh * P:lh * D + (dh + 1) * P], x1[:, dh, lh * P:(lh + 1) * P], idn[:]))
            if plain:
                xt_hi = free[0] = a(lambda: activate(gated[s][:], both, ACT.Copy), r)
            else:
                xt_hi = upper(one, both, r)
            yield
            xt_lo = lower(one, both, xt_hi)
            free[0] = xt_lo
            t = v(lambda: TT(den[s][:], den[s][:], cnt[:, q, :], ALU.mult), t2)
            t = v(lambda: V.reciprocal(den[s][:], den[s][:]), t)
            for j in range(2):
                t2 = v(lambda j=j: TS(prob[:, j, :], prob[:, j, :], den[s][:, j:j + 1], None, ALU.mult), t)
            yield
            if not plain:
                yield
            pe.wait(t2, free[0])
            for j in range(2):
                for lh in range(2):
                    r = pe.do(lambda lh=lh, j=j: nc.tensor.transpose(
                        ps[:, lh * S + j * P:lh * S + (j + 1) * P], prob[:, j, lh * P:(lh + 1) * P], idn[:]))
            if plain:
                pt_hi = a(lambda: activate(soma[s][:], both, ACT.Copy), r)
            else:
                pt_hi = upper(two, both, r)
            yield
            pt_lo = lower(two, both, pt_hi)
            free[0] = pt_lo
            yield
            pe.wait(xt_hi, xt_lo, pt_hi, pt_lo)
            for dh in range(DH):
                c = slice(dh * P, (dh + 1) * P)
                pooled = products(both[:, dh, :], passes(
                    [(one[0][:, lh, c], one[1][:, lh, c], gated[s][:, lh, c]) for lh in range(2)],
                    halves((soma[s], soma[s]) if plain else two)))
            t = v(lambda: TT(acc[b % NACC][:, :, tok], both, x1[:], ALU.add), pooled,
                  acc_stored[b - NACC] if b >= NACC else None)
            side_done[s] = t
            res_ready.setdefault(b, []).append(t)
            yield

        plan = []
        for e, blocks in RUNS:
            plan += [("head" if e == HEAD else "expert", blocks[0] if e == HEAD else e, c) for c in range(FC)]
        raw_in, raw_free, w_ready, w_free = {}, [None] * NRAW, {}, {}
        fetched, cut = [0], [0]
        we_here, we_free = {}, [None] * (2 * BB)

        def fetch():
            n = fetched[0]
            if n >= len(plan):
                return
            fetched[0] += 1
            kind, e, c = plan[n]
            sp.wait(raw_free[n % NRAW])
            dst, src = ((w_raw[n % NRAW][:], chunks[e, c]) if kind == "expert"
                        else (w_raw[n % NRAW][:, 0:HROW], head_chunks[c]))
            raw_in[n] = sp.do(lambda: nc.sync.dma_start(dst, src), s_raw[n % NRAW], 16)

        def gather(b):
            for s in range(BB):
                i, q = SLOT[b] * BB + s, b * BB + s
                pool.wait(late_marks["rows"], we_free[i])
                we_here[q] = pool.do(lambda q=q, i=i: nc.gpsimd.indirect_dma_start(
                    out=we_in[i][:], out_offset=None, in_=we_rows[:],
                    in_offset=bass.IndirectOffsetOnAxis(ap=ex_row[:, q:q + 1], axis=0)), s_we[i], 16)

        def cut_next():
            n = cut[0]
            cut[0] += 1
            k, raw = n % WSLOTS, w_raw[n % NRAW]
            kind, e, c = plan[n]
            arrived = [raw_in[n]]
            if kind == "expert":
                parts = [(slice(0, WROW), raw[:])]
            else:
                rest = raw[:, HROW - PART:HROW]
                routed = [we_in[SLOT[e] * BB + s][:, c * PART:(c + 1) * PART] for s in range(BB)]
                parts = [(slice(0, HROW), raw[:, 0:HROW]), (slice(HROW, HROW + PART), routed[0]),
                         (slice(HROW + PART, HROW + 2 * PART), rest),
                         (slice(HROW + 2 * PART, HROW + 3 * PART), routed[1])]
                arrived += [we_here[e * BB + s] for s in range(BB)]
            act.wait(w_free.get(n - WSLOTS), *arrived)
            for at, src in parts:
                hi = act.do(lambda at=at, src=src: activate(w_hi[k][:, at], src, ACT.Copy), s_whi)
            dve.wait(hi, w_free.get(n - WSLOTS), *arrived)
            for at, src in parts:
                lo = dve.do(lambda at=at, src=src: TT(w_lo[k][:, at], src, f(w_hi[k][:, at]), ALU.subtract), s_wlo)
            raw_free[n % NRAW] = lo
            if kind == "head" and c == FC - 1:
                for s in range(BB):
                    we_free[SLOT[e] * BB + s] = lo
                if e + 2 < NBLK:
                    gather(e + 2)
            w_ready[n] = (hi, lo)
            fetch()

        slot_marks, slot_free = {}, [None, None]
        gu_free = [[None, None], [None, None]]
        hid_free, hl_free, out_free = [None] * 3, [None] * DEPTH, [None]
        acc_done = {}
        step_no = [0]

        def split_residual(b, slot, marks):
            act.wait(slot_free[slot], *marks)
            hi = act.do(lambda: activate(res_hi[slot][:], acc[b % NACC][:], ACT.Copy), s_rhi)
            dve.wait(hi, slot_free[slot], *marks)
            lo = dve.do(lambda: TT(res_lo[slot][:], acc[b % NACC][:], f(res_hi[slot][:]), ALU.subtract), s_rlo)
            slot_marks[slot] = (hi, lo)

        class Step:

            def __init__(self, b, slot, c, n, last):
                self.b, self.slot, self.c, self.n, self.last = b, slot, c, n, last
                self.k = n % WSLOTS
                self.i = step_no[0]
                step_no[0] += 1

            def front_products(self, out, at):
                k, slot = self.k, self.slot
                cols = [slice(at + h * P, at + (h + 1) * P) for h in range(DH)]
                return products(out[:], exact([(w_hi[k][:, cols[h]], w_lo[k][:, cols[h]],
                                                res_hi[slot][:, h, :], res_lo[slot][:, h, :]) for h in range(DH)]), s_gu)

            def late(self):
                i, j = self.i % DEPTH, self.i % 3
                act.wait(self.hid, hl_free[i])
                self.hi = act.do(lambda: activate(hid_hi[i][:], hid[j][:], ACT.Copy), s_hhi)
                pool.wait(self.hi, self.hid, hl_free[i])
                self.lo = pool.do(lambda: nc.gpsimd.tensor_tensor(hid_lo[i][:], hid[j][:], f(hid_hi[i][:]),
                                                                  ALU.subtract), s_hlo)
                hid_free[j] = self.lo

            def back_products(self, out, weight, tok=slice(0, BT), clears=True, lone=True):
                hi, lo = hid_hi[self.i % DEPTH], hid_lo[self.i % DEPTH]
                return products(out, exact([(weight[0], weight[1], hi[:, tok], lo[:, tok])]), s_down,
                                start=self.c == 0 and clears, stop=self.c == FC - 1, lone=lone)

            def back(self):
                pe.wait(self.hi, self.lo)
                if self.c == 0:
                    pe.wait(out_free[0])
                m = self.down()
                hl_free[self.i % DEPTH] = m
                if self.last:
                    w_free[self.n] = m
                if self.c == FC - 1:
                    dve.wait(m, acc_done.get(self.b))
                    out_free[0] = acc_done[self.b] = self.close()

        class ExpertStep(Step):
            def __init__(self, e, *args):
                super().__init__(*args)
                self.e = e

            def front(self):
                i = self.i % 2
                pe.wait(*w_ready[self.n], *slot_marks[self.slot], *gu_free[i])
                self.gate = self.front_products(ps_gate[i], 0)
                self.up = self.front_products(ps_up[i], DH * P)
                slot_free[self.slot] = self.up

            def mid(self):
                i, h = self.i % 2, hid[self.i % 3][:]
                act.wait(self.gate, hid_free[self.i % 3])
                m = act.do(lambda: activate(h, ps_gate[i][:], ACT.Silu), s_act)
                dve.wait(m, self.up)
                self.hid = dve.do(lambda: TT(h, h, ps_up[i][:], ALU.mult), s_hid)
                gu_free[i] = [m, self.hid]

            def down(self):
                for h in range(DH):
                    c = slice(2 * DH * P + h * P, 2 * DH * P + (h + 1) * P)
                    m = self.back_products(ps_out[:, h, :], (w_hi[self.k][:, c], w_lo[self.k][:, c]))
                return m

            def close(self):
                X = acc[self.b % NACC]
                dve.wait(*slot_marks[self.slot])
                for s in range(BB):
                    q, tok = self.b * BB + s, slice(s * S, (s + 1) * S)
                    r = dve.do(lambda q=q, tok=tok: STT(X[:, :, tok], ps_out[:, :, tok], coef[:, self.e, q:q + 1],
                                                        X[:, :, tok], ALU.mult, ALU.add), s_acc)
                return r

        class HeadStep(Step):
            def front(self):
                i = self.i % 2
                pe.wait(*w_ready[self.n], *slot_marks[self.slot], *gu_free[i])
                self.pre = self.front_products(ps_gate[i], 0)
                slot_free[self.slot] = self.pre

            def mid(self):
                i, h = self.i % 2, hid[self.i % 3][:]
                act.wait(self.pre, hid_free[self.i % 3])
                self.hid = act.do(lambda: activate(h, ps_gate[i][:], ACT.Gelu,
                                                   bias=b1h[:, self.c:self.c + 1]), s_act)
                gu_free[i][0] = self.hid

            def down(self):
                hl = (w_hi[self.k], w_lo[self.k])
                self.back_products(ps_out[:, 0, :], [t[:, DH * P:(DH + 1) * P] for t in hl])
                for s in range(BB):
                    w = [t[:, (DH + 1 + s) * P:(DH + 2 + s) * P] for t in hl]
                    tok = slice(s * S, (s + 1) * S)
                    m = self.back_products(ps_out[:, 1, tok], w, tok, clears=s == 0, lone=False)
                return m

            def close(self):
                b = self.b
                X = acc[b % NACC]
                dve.wait(*slot_marks[self.slot])
                r = dve.do(lambda: STT(X[:, 0, :], ps_out[:, 0, :], b2a, X[:, 0, :], ALU.add, ALU.add), s_acc)
                for s in range(BB):
                    q, tok = b * BB + s, slice(s * S, (s + 1) * S)
                    r = dve.do(lambda q=q, tok=tok: STT(X[:, 1, tok], ps_out[:, 1, tok], bias_b[:, q:q + 1],
                                                        X[:, 1, tok], ALU.add, ALU.add), s_acc)
                sp.wait(r)
                acc_stored[b] = sp.do(lambda: nc.sync.dma_start(y_blk[:, :, b * BT:(b + 1) * BT], X[:]),
                                      s_y[b % NACC], 16)
                return r

        for _ in range(NRAW):
            fetch()
        ready.update({0: [side_in[0]], 4: [side_in[4 * D]], 8: [side_in[8 * D]]})
        for i, _ in enumerate(zip(*[layers01(0, s) for s in range(BB)])):
            if i == 0:
                next(setting_up)
                split_8 = next(splitting)
            elif i == 1:
                ready["small"] = next(setting_up)
                ready["blend"] = setup_blend()
                split_4 = next(splitting)
            elif i == 2:
                split_0 = next(splitting)
            elif i == 5:
                setting_late = setup_late()
                late_marks["rows"] = next(setting_late)
            elif i == 9:
                late_marks["done"] = next(setting_late)
                ready[8] += split_8
                ready[4] += split_4
                ready[0] += split_0
            elif i > FIRST_CUT and cut[0] < WSLOTS:
                cut_next()
            elif cut[0] == WSLOTS and not we_here:
                gather(0)
                gather(1)
        for lane in (pe, act, dve, pool):
            lane.wait(late_marks["done"])

        queue = []
        occupant = [None, None]
        final = {}
        experts_left = [NE + 1] * NBLK
        def later_blocks(s):
            for b in range(1, NBLK):
                yield from layers01(b, s)

        first, second = later_blocks(0), later_blocks(1)
        side = {"rate": 0.0, "due": 0.0}

        def side_piece():
            made[0] += 1
            next(first, None)
            if made[0] > BEHIND:
                next(second, None)

        def some_side_work():
            side["due"] += side["rate"]
            if side["due"] >= 1.0:
                side["due"] -= 1.0
                side_piece()

        to_split = [[(b, kind) for b in range(NBLK) if SLOT[b] == slot for kind in ("experts", "head")]
                    for slot in range(2)]

        def split_ready(force=False):
            for slot, turns in enumerate(to_split):
                if not turns:
                    continue
                b, kind = turns[0]
                if kind == "experts":
                    if occupant[slot] is not None or len(res_ready.get(b, ())) < BB:
                        continue
                    occupant[slot] = b
                    split_residual(b, slot, res_ready[b])
                else:
                    if b not in final or (step_no[0] < final[b] + 2 and not force):
                        continue
                    split_residual(b, slot, [acc_done[b]])
                split_kinds.add(turns.pop(0))

        split_kinds = set()

        def run(step, kind):
            split_ready()
            if (step.b, kind) not in split_kinds:
                finish()
                split_ready(force=True)
            step.front()
            step.mid()
            if kind == "head" and step.c == FC - 1:
                occupant[step.slot] = None
            queue.append(step)
            if len(queue) > 1:
                queue[-2].late()
            if len(queue) > DEPTH:
                back()
            while cut[0] < len(plan) and cut[0] - WSLOTS in w_free:
                cut_next()
            some_side_work()

        def back():
            step = queue.pop(0)
            step.back()
            if isinstance(step, ExpertStep) and step.c == FC - 1:
                experts_left[step.b] -= 1
                if not experts_left[step.b]:
                    final[step.b] = step_no[0]

        def finish():
            if queue:
                queue[-1].late()
            while queue:
                back()

        def pieces_per_step(r):
            best, steps = 0.0, 0
            for k in range(r, len(RUNS)):
                e, blocks = RUNS[k]
                need = PIECES * max(blocks) + BEHIND - made[0] if max(blocks) else 0
                if k > r:
                    best = max(best, need / max(1, steps - 3))
                steps += 0 if quiet_run(k) else FC * len(blocks)
            return min(1.0, best)

        def quiet_run(k):
            return RUNS[k][0] == HEAD

        made = [0]
        split_ready()
        for r, (e, blocks) in enumerate(RUNS):
            while len(res_ready.get(blocks[-1], ())) < BB:
                side_piece()
            side["rate"] = 0.0 if quiet_run(r) else pieces_per_step(r)
            for b in blocks:
                for c in range(FC):
                    if e == HEAD:
                        run(HeadStep(b, SLOT[b], c, r * FC + c, True), "head")
                    else:
                        run(ExpertStep(e, b, SLOT[b], c, r * FC + c, b == blocks[-1]), "experts")
        finish()
        for b in range(NBLK):
            sp.wait(acc_stored[b])

        block = ctx.enter_context(nc.Block())

        @block.sync
        def _(eng):
            for w in sp.work:
                w(eng)

        @block.tensor
        def _(eng):
            for w in pe.work:
                w(eng)

        @block.vector
        def _(eng):
            for w in dve.work:
                w(eng)

        @block.scalar
        def _(eng):
            for w in act.work:
                w(eng)

        @block.gpsimd
        def _(eng):
            for w in pool.work:
                w(eng)


def kernel(**inputs):
    import numpy as np
    import concourse.bacc as bacc
    from concourse.bass_utils import run_bass_kernel_spmd

    g = {k: np.asarray(v) for k, v in inputs.items()}

    def rows(w):
        k = w.shape[0] // P
        return np.ascontiguousarray(w.reshape(k, P, -1).transpose(1, 0, 2)).reshape(P, -1)

    def cols(v):
        return v.reshape(-1, P).T

    def chunk_rows(gate, up, down):
        first = [w.reshape(DH, P, FC, P).transpose(2, 1, 0, 3).reshape(FC, P, DH * P) for w in (gate, up)]
        return np.concatenate(first + [down.reshape(FC, P, D)], axis=2)

    gs = [chunk_rows(g["L2_cond_Wg"][e], g["L2_cond_Wu"][e], g["L2_cond_Wd"][e]) for e in range(NE)]
    gs.append(chunk_rows(g["L2_cond_Sg"], g["L2_cond_Su"], g["L2_cond_Sd"]))
    w1 = g["L3_cond_W1"].reshape(DH, P, FC, P).transpose(2, 1, 0, 3).reshape(FC, P, DH * P)
    w2 = g["L3_cond_W2"].reshape(FC, P, NSH)
    head = np.concatenate([w1, w2], axis=2)
    f32 = np.float32
    j = np.arange(S).reshape(2, P).T
    key = np.arange(S)
    masks = np.stack([key > j[:, :, None], key < j[:, :, None]], 1).astype(f32)
    jcount = np.concatenate([j + 1, S - j, np.full((P, 1), S - 1)], 1).astype(f32)
    be_pad = np.zeros((NE, P), f32)
    be_pad[:, PART:] = g["L3_cond_be"]
    b2 = g["L3_cond_b2"]
    b2b = np.zeros((P,), f32)
    b2b[:PART] = b2[P:]
    arrays = {
        "xT": g["x"].reshape(T, D).T,
        "chunks": np.stack(gs),
        "head_chunks": head,
        "sidew": np.concatenate([rows(g["L0_cond_Wg"].T), rows(g["L0_cond_Wtemp"].T), rows(g["L0_cond_Wsoma"].T),
                                 rows(g["L0_cond_Wout"].T), rows(g["L0_cond_Wn1"].T), rows(g["L1_cond_W1"])], 1),
        "vec128": np.concatenate([cols(g[n]) for n in ("L0_cond_bg", "L0_cond_bsoma", "L0_cond_btemp",
                                                       "L0_cond_gamma", "L0_cond_beta", "L3_cond_b1")]
                                 + [b2[:P, None], b2b[:, None]], 1),
        "w64": np.concatenate([g["cond_256"].T, g["L0_cond_bn1"][:, None], g["L1_cond_b1"][:, None],
                               g["L1_cond_v"][:, None]], 1),
        "vec16": g["condB_bn2"][:, None],
        "masks": masks,
        "ident": np.eye(P, dtype=f32),
        "we_rows": g["L3_cond_We"].reshape(NE, FC, P, PART).transpose(0, 2, 1, 3).reshape(NE * P, FC * PART),
        "be_pad": be_pad,
        "blendT": rows(g["cond_1024"].T).reshape(P, DH, ND),
        "taus": np.concatenate([g["condB_tauraws"], g["L0_cond_tau_ctx"].reshape(1)]),
        "types": g["itok_B_0_2"],
        "experts": g["itok_B_0_7"],
        "gates": g["fside_Bx8_0"],
        "shared_gate": g["condB_sharedgateprob"],
        "jcount": jcount,
        "prow": np.arange(P, dtype=f32)[:, None],
    }
    nc = bacc.Bacc("TRN2", target_bir_lowering=False, num_devices=1)
    maps, args = {}, []
    for name, arr in arrays.items():
        arr = np.ascontiguousarray(arr)
        maps[f"in_{name}"] = arr
        args.append(nc.dram_tensor(f"in_{name}", arr.shape, mybir.dt.from_np(arr.dtype), kind="ExternalInput").ap())
    args.append(nc.dram_tensor("out_yT", (D, T), mybir.dt.float32, kind="ExternalOutput").ap())
    residual_stack_kernel(nc, *args)
    r = run_bass_kernel_spmd(nc, [maps], core_ids=[0])
    return np.ascontiguousarray(r.results[0]["out_yT"].T).reshape(B, S, D)
```
